# Optimizing a Trainium2 kernel written in Bass

```python
import numpy as np
import jax
import jax.numpy as jnp

def _softmax(x, axis=-1):
    return jax.nn.softmax(x, axis=axis)

def _gelu(x):
    return jax.nn.gelu(x, approximate=True)

def _silu(x):
    return jax.nn.silu(x)

def _sigmoid(x):
    return jax.nn.sigmoid(x)

def _layernorm(x, axis=-1, eps=1e-05):
    m = jnp.mean(x, axis=axis, keepdims=True)
    v = jnp.var(x, axis=axis, keepdims=True)
    return (x - m) / jnp.sqrt(v + eps)

def _scatter_add(tgt, idx, src, axis=0):
    return tgt.at[idx].add(src)

def _segment_sum(src, seg, n):
    return jax.ops.segment_sum(src, seg, n)
kernel_name = 'mk_macaron_d1_jaxref_r8_b4aebe'

def setup_inputs(seed: int=0):
    np.random.seed(seed)
    _w = jnp.asarray

    def _L0_attn_setup():
        import jax, jax.numpy as jnp
        import numpy as np
        EMBED_DIM = 128
        NUM_HEADS = 16
        HEAD_DIM = EMBED_DIM // NUM_HEADS
        FEATURE_EPS = 1e-06
        DEN_EPS = 1e-06
        key = jax.random.key(seed)
        k_x, k_qw, k_qb, k_ow, k_ob = jax.random.split(key, 5)
        b, l = (2, 256)
        x = jax.random.normal(k_x, (b, l, EMBED_DIM), dtype=jnp.float32)
        s = 1.0 / np.sqrt(EMBED_DIM)
        qkv_w = jax.random.uniform(k_qw, (3 * EMBED_DIM, EMBED_DIM), minval=-s, maxval=s, dtype=jnp.float32)
        qkv_b = jax.random.uniform(k_qb, (3 * EMBED_DIM,), minval=-s, maxval=s, dtype=jnp.float32)
        out_w = jax.random.uniform(k_ow, (EMBED_DIM, EMBED_DIM), minval=-s, maxval=s, dtype=jnp.float32)
        out_b = jax.random.uniform(k_ob, (EMBED_DIM,), minval=-s, maxval=s, dtype=jnp.float32)
        return {'x': x, 'qkv_w': qkv_w, 'qkv_b': qkv_b, 'out_w': out_w, 'out_b': out_b}
    _L0_attn_in = _L0_attn_setup()

    def _L0_ffn_setup():
        import jax, jax.numpy as jnp
        import numpy as np
        B, S, DIM = (4, 256, 128)
        INTER = int(int(DIM * 4) * 0.25)
        E = 32 - 1
        K = 4 - 1

        def _gelu(t):
            return jax.nn.gelu(t, approximate=False)
        key = jax.random.key(seed)
        ks = jax.random.split(key, 12)
        s = 0.02
        return {'x': jax.random.normal(ks[0], (B, S, DIM), jnp.float32), 'ws1': jax.random.normal(ks[1], (DIM, INTER), jnp.float32) * s, 'bs1': jnp.zeros((INTER,), jnp.float32), 'ws2': jax.random.normal(ks[2], (INTER, DIM), jnp.float32) * s, 'bs2': jnp.zeros((DIM,), jnp.float32), 'We1': jax.random.normal(ks[3], (E, DIM, INTER), jnp.float32) * s, 'Be1': jnp.zeros((E, INTER), jnp.float32), 'We2': jax.random.normal(ks[4], (E, INTER, DIM), jnp.float32) * s, 'Be2': jnp.zeros((E, DIM), jnp.float32), 'Wr': jax.random.normal(ks[5], (DIM, E), jnp.float32) * s, 'br': jnp.zeros((E,), jnp.float32)}
    _L0_ffn_in = _L0_ffn_setup()
    _d = {'L0_attn_x': _L0_attn_in['x'], 'L0_attn_qkv_w': _L0_attn_in['qkv_w'], 'L0_attn_qkv_b': _L0_attn_in['qkv_b'], 'L0_attn_out_w': _L0_attn_in['out_w'], 'L0_attn_out_b': _L0_attn_in['out_b'], 'L0_ffn_ws1': _L0_ffn_in['ws1'], 'L0_ffn_bs1': _L0_ffn_in['bs1'], 'L0_ffn_ws2': _L0_ffn_in['ws2'], 'L0_ffn_bs2': _L0_ffn_in['bs2'], 'L0_ffn_We1': _L0_ffn_in['We1'], 'L0_ffn_Be1': _L0_ffn_in['Be1'], 'L0_ffn_We2': _L0_ffn_in['We2'], 'L0_ffn_Be2': _L0_ffn_in['Be2'], 'L0_ffn_Wr': _L0_ffn_in['Wr'], 'L0_ffn_br': _L0_ffn_in['br']}
    _x0 = _d['L0_attn_x']
    _d['L0_attn_x'] = jax.random.normal(jax.random.fold_in(jax.random.key(seed), 1), (4, 1024, 128), dtype=_x0.dtype)
    del _x0
    return _d

def reference(L0_attn_x, L0_attn_qkv_w, L0_attn_qkv_b, L0_attn_out_w, L0_attn_out_b, L0_ffn_ws1, L0_ffn_bs1, L0_ffn_ws2, L0_ffn_bs2, L0_ffn_We1, L0_ffn_Be1, L0_ffn_We2, L0_ffn_Be2, L0_ffn_Wr, L0_ffn_br):

    def _L0_attn_ref(x, qkv_w, qkv_b, out_w, out_b):
        import jax, jax.numpy as jnp
        import numpy as np
        EMBED_DIM = 128
        NUM_HEADS = 16
        HEAD_DIM = EMBED_DIM // NUM_HEADS
        FEATURE_EPS = 1e-06
        DEN_EPS = 1e-06
        b, l, e = x.shape
        qkv = (x @ qkv_w.T + qkv_b).reshape(b, l, 3, NUM_HEADS, HEAD_DIM)
        qkv = jnp.transpose(qkv, (2, 0, 3, 1, 4))
        q, k, v = (qkv[0], qkv[1], qkv[2])
        q = jax.nn.relu(q) + FEATURE_EPS
        k = jax.nn.relu(k) + FEATURE_EPS
        kv = jnp.cumsum(jnp.einsum('bhld,bhle->bhlde', k, v), axis=2)
        k_cum = jnp.cumsum(k, axis=2)
        num = jnp.einsum('bhld,bhlde->bhle', q, kv)
        den = jnp.maximum(jnp.einsum('bhld,bhld->bhl', q, k_cum)[..., None], DEN_EPS)
        out = num / den
        out = jnp.transpose(out, (0, 2, 1, 3)).reshape(b, l, e)
        return out @ out_w.T + out_b

    def _L0_ffn_ref(x, ws1, bs1, ws2, bs2, We1, Be1, We2, Be2, Wr, br):
        import jax, jax.numpy as jnp
        import numpy as np
        B, S, DIM = (4, 256, 128)
        INTER = int(int(DIM * 4) * 0.25)
        E = 32 - 1
        K = 4 - 1

        def _gelu(t):
            return jax.nn.gelu(t, approximate=False)
        shared = _gelu(x @ ws1 + bs1) @ ws2 + bs2
        aff = jax.nn.softmax(x @ Wr + br, axis=-1)
        vals, idx = jax.lax.top_k(aff, K)
        gates = jnp.sum(jax.nn.one_hot(idx, E, dtype=x.dtype) * vals[..., None], axis=-2)
        gates_e = jnp.moveaxis(gates, -1, 0)

        def step(acc, p):
            W1, B1, W2, B2, g = p
            h = _gelu(x @ W1 + B1)
            return (acc + g[..., None] * (h @ W2 + B2), None)
        routed, _ = jax.lax.scan(step, jnp.zeros_like(x), (We1, Be1, We2, Be2, gates_e))
        return shared + routed + x
    x = L0_attn_x
    x = x + 0.5 * _L0_ffn_ref(_layernorm(x, axis=-1), L0_ffn_ws1, L0_ffn_bs1, L0_ffn_ws2, L0_ffn_bs2, L0_ffn_We1, L0_ffn_Be1, L0_ffn_We2, L0_ffn_Be2, L0_ffn_Wr, L0_ffn_br)
    x = x + _L0_attn_ref(_layernorm(x, axis=-1), L0_attn_qkv_w, L0_attn_qkv_b, L0_attn_out_w, L0_attn_out_b)
    x = x + 0.5 * _L0_ffn_ref(_layernorm(x, axis=-1), L0_ffn_ws1, L0_ffn_bs1, L0_ffn_ws2, L0_ffn_bs2, L0_ffn_We1, L0_ffn_Be1, L0_ffn_We2, L0_ffn_Be2, L0_ffn_Wr, L0_ffn_br)
    return x

_drawn_inputs = setup_inputs


def setup_inputs(seed=0):
    import zlib

    import numpy as np

    out = dict(_drawn_inputs(seed))
    spreads = {'L0_ffn_bs1': (0.0, 0.8),
     'L0_ffn_bs2': (0.0, 0.1),
     'L0_ffn_Be1': (0.0, 0.8),
     'L0_ffn_Be2': (0.0, 0.8),
     'L0_ffn_br': (0.0, 0.8)}
    factors = {'L0_ffn_ws1': 3.602,
     'L0_ffn_ws2': 3.236,
     'L0_ffn_We1': 8.0,
     'L0_ffn_We2': 8.0,
     'L0_ffn_Wr': 8.0}
    for name, (base, spread) in spreads.items():
        noise = np.random.default_rng([zlib.crc32(name.encode()), seed]).standard_normal(out[name].shape)
        drawn = base * np.exp(spread * noise) if base else spread * noise
        out[name] = jnp.asarray(drawn.astype(out[name].dtype))
    for name, factor in factors.items():
        out[name] = (out[name] * factor).astype(out[name].dtype)
    return out
```

```python
from contextlib import ExitStack

import concourse.bass as bass
from concourse import mybir

F32 = mybir.dt.float32
BF16 = mybir.dt.bfloat16
I32 = mybir.dt.int32
U32 = mybir.dt.uint32
ALU = mybir.AluOpType
ACT = mybir.ActivationFunctionType
AXX = mybir.AxisListType.X

P = 128
LN_EPS = 1e-5
FEATURE_EPS = 1e-6
DEN_EPS = 1e-6
RSQRT_SEED = 0x5F3759DF


def macaron_kernel(nc, x_in, qkv_w, qkv_b, out_w, out_b, ws1, bs1, ws2, bs2,
                   we1, be1, we2, be2, wr, br, out):
    BATCH, SEQ, D = x_in.shape
    E, _, F = we1.shape
    TOPK = 3
    HEADS, HD = 16, D // 16
    HA = HD + 1
    TILES = BATCH * SEQ // P
    GROUPS = 2
    GT = TILES // GROUPS
    BT = SEQ // P
    QUADS = GT // 4
    PAIRS = GT * P * TOPK
    SLOT_TILES = PAIRS // P - 1 + E
    CH = 3
    CHUNKS = SLOT_TILES // CH
    RING = 4
    RP = 32
    W_COLS = 2 * F + 1
    assert D == P and F == P and SLOT_TILES % CH == 0 and (CHUNKS - 2) % RING == 0
    HEAD_CUTS = [(0, 6), (6, 11), (11, 16)]

    x_tok = x_in.rearrange("b (t p) d -> p (b t) d", p=P)
    out_tok = out.rearrange("b (t p) d -> p (b t) d", p=P)
    def scratch(name):
        rows = [nc.dram_tensor(f"{name}{g}", [SLOT_TILES * P, D], F32, kind="Internal").ap() for g in range(GROUPS)]
        return rows, [r.rearrange("(c u p) d -> p c u d", u=CH, p=P) for r in rows]

    xs_rows, xs_chunks = scratch("xs_rows")
    ys_rows, ys_chunks = scratch("ys_rows")

    with ExitStack() as ctx:
        def sb(name, shape, dt=F32):
            return ctx.enter_context(nc.sbuf_tensor(name, shape, dt))

        def sem(name):
            return ctx.enter_context(nc.semaphore(name))

        bank = [ctx.enter_context(nc.psum_tensor(f"bank{i}", [P, 512], F32)) for i in range(8)]

        experts = sb("experts", [P, E, W_COLS])
        be1_rows = sb("be1_rows", [E, F])
        be2_aug = sb("be2_aug", [P, 4, D])
        wr_sb = sb("wr_sb", [P, E])
        br_all = sb("br_all", [P, E])
        ws1_sb = sb("ws1_sb", [P, F])
        ws2_sb = sb("ws2_sb", [P, D])
        bs1_col = sb("bs1_col", [P, 1])
        attn_rows = sb("attn_rows", [P, 4, D])
        attn_wT = sb("attn_wT", [P, 4, D])
        qkv_bias = sb("qkv_bias", [1, 3 * D])
        out_bias = sb("out_bias", [1, D])
        ident = sb("ident", [P, P])
        tri = sb("tri", [P, P])
        ones_row = sb("ones_row", [1, P])
        before = sb("before", [P, P], BF16)
        ones = sb("ones", [P, P], BF16)
        head_mask = sb("head_mask", [P, HEADS, HA])
        expert_ids = sb("expert_ids", [P, E])
        row_id = sb("row_id", [P, 1])

        x = sb("x", [P, TILES, D])
        xn = sb("xn", [P, TILES, D])
        xnT = sb("xnT", [P, GT * P])
        sharedT = sb("sharedT", [P, GT * P])
        stats = sb("stats", [P, GT, 6])
        mean = sb("mean", [P, GT])
        var = sb("var", [P, GT])
        rstd = sb("rstd", [P, GT])
        tmp_a = sb("tmp_a", [P, GT])
        tmp_b = sb("tmp_b", [P, GT])
        seed = sb("seed", [P, GT], I32)
        seed_f = sb("seed_f", [P, GT])
        logits = sb("logits", [P, GT, RP])
        probs = sb("probs", [P, GT, RP])
        row_max = sb("row_max", [P, GT])
        row_sum = sb("row_sum", [P, GT])
        top = sb("top", [P, GT, 8])
        top_id = sb("top_id", [P, GT, 8], U32)
        top_idf = sb("top_idf", [P, GT, TOPK])
        one_hot = sb("one_hot", [P, GT, TOPK, E])
        hot_slots = sb("hot_slots", [P, GT, TOPK, E])
        chosen_a = sb("chosen_a", [P, GT, E])
        chosen = sb("chosen", [P, GT, E], BF16)
        gates = sb("gates", [P, GT, RP])
        gatesT = sb("gatesT", [P, QUADS, P])
        half_gate = sb("half_gate", [P, TILES, TOPK])
        count_i = sb("count_i", [P, E], I32)
        count_t = sb("count_t", [P, E], I32)
        run_tiles = sb("run_tiles", [P, E])
        run_end = sb("run_end", [P, E])
        run_base = sb("run_base", [P, E])
        zero_row = sb("zero_row", [P, E])
        slot_of = sb("slot_of", [P, GT, E])
        slot_f = sb("slot_f", [P, GT, TOPK])
        slots = sb("slots", [P, TILES, TOPK], U32)
        ended = sb("ended", [P, E])
        tile_expert = sb("tile_expert", [P, 1])
        expert_tab = sb("expert_tab", [1, GROUPS * P], I32)
        y_tok = sb("y_tok", [P, TILES, TOPK, D])

        xs_in = sb("xs_in", [P, RING, CH, D])
        xsT = sb("xsT", [P, 2, CH * P])
        w_ring = sb("w_ring", [P, RING, CH, W_COLS])
        hT = sb("hT", [P, 2, CH * P])
        ys_out = sb("ys_out", [P, RING, CH, D])

        zeros = ys_out[:, 0, :, :]

        xaT = sharedT[:, 0:2 * 4 * P].rearrange("p (b n) -> p b n", b=2)
        xa = sharedT[:, 2 * 4 * P:3 * 4 * P].rearrange("p (t d) -> p t d", d=D)
        qk = sb("qk", [P, 2, 2 * D])
        v_aug = sb("v_aug", [P, 2, HEADS, HA])
        kv = w_ring[:].rearrange("p r u w -> p (r u w)")[:, 0:2 * HEADS * HA * HD].rearrange(
            "p (b h e d) -> p b h e d", b=2, e=HA, d=HD)
        weighed = hot_slots[:].rearrange("p t k e -> p (t k e)")[:, 0:HEADS * HA * HD].rearrange(
            "p (h e d) -> p h e d", e=HA, d=HD)
        num_den = sb("num_den", [P, HEADS, HA])
        den = sb("den", [P, HEADS])
        den_inv = sb("den_inv", [P, HEADS])
        attn_o = sb("attn_o", [P, D])
        q_oT = sb("q_oT", [P, 2, P])
        state = sb("state", [P, HEADS * HA])

        x_loaded = [sem(f"x_loaded{g}") for g in range(GROUPS)]
        router_w_loaded = sem("router_w_loaded")
        attn_w_loaded = sem("attn_w_loaded")
        experts_loaded = sem("experts_loaded")
        zeros_made = sem("zeros_made")
        slots_zeroed = sem("slots_zeroed")
        consts_made = sem("consts_made")
        pool_step = sem("pool_step")
        dve_step = sem("dve_step")
        w_transposed = sem("w_transposed")
        xn_ready = sem("xn_ready")
        xn_transposed = sem("xn_transposed")
        xnT_ready = sem("xnT_ready")
        logits_done = sem("logits_done")
        exp_asked = sem("exp_asked")
        exp_done = sem("exp_done")
        chosen_ready = sem("chosen_ready")
        gates_ready = sem("gates_ready")
        ranks_done = sem("ranks_done")
        slots_ready = sem("slots_ready")
        tile_expert_ready = sem("tile_expert_ready")
        expert_row_done = sem("expert_row_done")
        shared_h_done = sem("shared_h_done")
        sharedT_ready = sem("sharedT_ready")
        gates_transposed = sem("gates_transposed")
        gatesT_ready = sem("gatesT_ready")
        shared_out_done = sem("shared_out_done")
        shared_out_read = sem("shared_out_read")
        router_done = sem("router_done")
        xs_scattered = [sem(f"xs_scattered{g}") for g in range(GROUPS)]
        xs_loaded = [sem(f"xs_loaded{r}") for r in range(RING)]
        xs_transposed = sem("xs_transposed")
        xsT_ready = sem("xsT_ready")
        weights_copied = sem("weights_copied")
        h_done = sem("h_done")
        hT_ready = sem("hT_ready")
        y_done = sem("y_done")
        ys_ready = sem("ys_ready")
        ys_stored = [sem(f"ys_stored{r}") for r in range(RING)]
        y_gathered = [sem(f"y_gathered{r}") for r in range(2)]
        xa_ready = sem("xa_ready")
        xa_transposed = sem("xa_transposed")
        xaT_ready = sem("xaT_ready")
        qkv_done = sem("qkv_done")
        qk_ready = sem("qk_ready")
        v_ready = sem("v_ready")
        kv_ready = sem("kv_ready")
        sums_done = sem("sums_done")
        sums_read = sem("sums_read")
        state_done = sem("state_done")
        state_ready = sem("state_ready")
        attn_o_ready = sem("attn_o_ready")
        q_o_transposed = sem("q_o_transposed")
        q_oT_ready = sem("q_oT_ready")
        in_out_done = sem("in_out_done")
        in_out_read = sem("in_out_read")
        x_final = sem("x_final")
        out_stored = sem("out_stored")

        N_ROUTER_W = 6 + 8
        N_ATTN_W = 4
        N_EXPERT_W = 3

        def stored_before(c):
            return [(c - r + RING - 1) // RING for r in range(RING)]

        def chunk_steps(eng, q, step):
            first = q * CHUNKS
            for c in range(2):
                step(first + c, 0, c == 0, False)
            loops = (CHUNKS - 2) // RING - 1
            with eng.Fori(0, loops) as i:
                for c in range(RING):
                    step(first + 2 + c, i, False, False)
            for c in range(2 + RING * loops, CHUNKS):
                step(first + c, 0, False, c == CHUNKS - 1)

        def wait_chunks(eng, semaphore, n, i, each=1):
            if isinstance(i, int):
                if n + RING * i > 0:
                    eng.wait_ge(semaphore, each * (n + RING * i))
            else:
                eng.wait_ge(semaphore, i * (RING * each) + each * n)

        block = ctx.enter_context(nc.Block())

        @block.sync
        def _(sp):
            def load(dst, src, done):
                sp.dma_start(dst, src).then_inc(done, 16)

            sp.wait_ge(zeros_made, 2)
            for g in range(GROUPS):
                load(x[:, g * GT:(g + 1) * GT, :], x_tok[:, g * GT:(g + 1) * GT, :], x_loaded[g])
                if g == 0:
                    load(wr_sb[:], wr, router_w_loaded)
                    load(br_all[:], br.unsqueeze(0).broadcast_to([P, E]), router_w_loaded)
                    load(ws1_sb[:], ws1, router_w_loaded)
                    load(ws2_sb[:], ws2, router_w_loaded)
                    load(bs1_col[:], bs1.unsqueeze(1), router_w_loaded)
                    load(be1_rows[:], be1, router_w_loaded)
                    for j in range(4):
                        load(be2_aug[RP * j:RP * j + E, j, :], be2, router_w_loaded)
                        load(be2_aug[RP * j + E:RP * j + RP, j, :], bs2.unsqueeze(0), router_w_loaded)
            for g in range(GROUPS):
                for c in range(CHUNKS):
                    sp.dma_start(xs_chunks[g][:, c, :, :], zeros).then_inc(slots_zeroed, 16)
            load(experts[:, :, 0:F], we1.rearrange("e d f -> d e f"), experts_loaded)
            load(experts[:, :, F:2 * F], we2.rearrange("e f d -> f e d"), experts_loaded)
            load(attn_rows[:, 0:3, :], qkv_w.rearrange("(c p) d -> p c d", p=P), attn_w_loaded)
            load(attn_rows[:, 3, :], out_w, attn_w_loaded)
            load(qkv_bias[:], qkv_b.unsqueeze(0), attn_w_loaded)
            load(out_bias[:], out_b.unsqueeze(0), attn_w_loaded)

            def experts_io(q):
                g = q % GROUPS
                sp.wait_ge(xs_scattered[g], 16 * GT * TOPK * (q // GROUPS + 1))

                def dram(chunks, C, i):
                    c = C - q * CHUNKS
                    if isinstance(i, int):
                        return chunks[g][:, c + RING * i, :, :]
                    return chunks[g][:, bass.ds(i * RING + c, 1), :, :].rearrange("p c u d -> p (c u) d")

                def load_chunk(C, i):
                    wait_chunks(sp, xs_transposed, C - RING + 1, i)
                    sp.dma_start(xs_in[:, C % RING, :, :], dram(xs_chunks, C, i)).then_inc(xs_loaded[C % RING], 16)

                def step(C, i, head, tail):
                    if head:
                        for c in range(3):
                            load_chunk(C + c, i)
                    if C - q * CHUNKS + 3 + (RING * i if isinstance(i, int) else 0) < CHUNKS:
                        load_chunk(C + 3, i)
                    wait_chunks(sp, ys_ready, C + 1, i)
                    sp.dma_start(dram(ys_chunks, C, i), ys_out[:, C % RING, :, :]).then_inc(ys_stored[C % RING], 16)

                chunk_steps(sp, q, step)

            experts_io(0)
            experts_io(1)
            experts_io(2)
            experts_io(3)
            for j in range(TILES // 4):
                sp.wait_ge(x_final, j + 1)
                sp.dma_start(out_tok[:, 4 * j:4 * j + 4, :], x[:, 4 * j:4 * j + 4, :]).then_inc(out_stored, 16)
            sp.wait_ge(out_stored, 16 * (TILES // 4))

        @block.gpsimd
        def _(pool):
            pool.memset(be2_aug[:], 0.0).then_inc(zeros_made, 1)
            pool.memset(zeros, 0.0).then_inc(zeros_made, 1)
            made = [0]

            def link(ins):
                made[0] += 1
                ins.then_inc(pool_step, 1)
                pool.wait_ge(pool_step, made[0])

            pool.memset(ident[:], 0.0)
            pool.memset(tri[:], 1.0)
            pool.memset(before[:], 1.0)
            pool.memset(ones[:], 1.0)
            pool.memset(ones_row[:], 1.0)
            pool.memset(head_mask[:], 1.0)
            pool.memset(zero_row[:], 0.0)
            pool.memset(v_aug[:], 1.0)
            pool.memset(gates[:], 1.0)
            pool.iota(expert_ids[:], [[1, E]], base=0, channel_multiplier=0, allow_small_or_imprecise_dtypes=True)
            link(pool.iota(row_id[:], [[1, 1]], base=0, channel_multiplier=1, allow_small_or_imprecise_dtypes=True))
            pool.affine_select(out=ident[:], in_=ident[:], compare_op=ALU.not_equal, fill=1.0, base=0,
                               pattern=[[-1, P]], channel_multiplier=1)
            pool.affine_select(out=tri[:], in_=tri[:], compare_op=ALU.is_ge, fill=0.0, base=0,
                               pattern=[[1, P]], channel_multiplier=-1)
            pool.affine_select(out=before[:], in_=before[:], compare_op=ALU.is_ge, fill=0.0, base=-1,
                               pattern=[[1, P]], channel_multiplier=-1)
            link(pool.affine_select(out=head_mask[:], in_=head_mask[:], compare_op=ALU.is_ge, fill=0.0, base=0,
                                    pattern=[[-HD, HEADS], [0, HA]], channel_multiplier=1))
            pool.affine_select(out=head_mask[:], in_=head_mask[:], compare_op=ALU.is_ge, fill=0.0, base=HD - 1,
                               pattern=[[HD, HEADS], [0, HA]], channel_multiplier=-1).then_inc(consts_made, 1)
            pool.wait_ge(slots_zeroed, 16 * GROUPS * CHUNKS)

            def scatter(q):
                g = q % GROUPS
                pool.wait_ge(slots_ready, q + 1)
                for t in range(g * GT, (g + 1) * GT):
                    for k in range(TOPK):
                        pool.indirect_dma_start(xs_rows[g], bass.IndirectOffsetOnAxis(slots[:, t, k:k + 1], 0),
                                                xn[:, t, :], None).then_inc(xs_scattered[g], 16)

            def gather(q):
                g = q % GROUPS
                for r, n in enumerate(stored_before((q + 1) * CHUNKS)):
                    pool.wait_ge(ys_stored[r], 16 * n)
                for j in range(QUADS):
                    n = q * QUADS + j
                    if n >= 2:
                        pool.wait_ge(y_gathered[n % 2], 16 * 4 * TOPK * (n // 2))
                    for t in range(g * GT + 4 * j, g * GT + 4 * j + 4):
                        for k in range(TOPK):
                            pool.indirect_dma_start(y_tok[:, t, k, :], None, ys_rows[g],
                                                    bass.IndirectOffsetOnAxis(slots[:, t, k:k + 1], 0)
                                                    ).then_inc(y_gathered[n % 2], 16)

            for layer in range(2):
                for g in range(GROUPS):
                    scatter(layer * GROUPS + g)
                for g in range(GROUPS):
                    gather(layer * GROUPS + g)

        @block.scalar
        def _(act):
            def copy(dst, src):
                return act.activation(dst, src, ACT.Copy)

            act.wait_ge(w_transposed, 1)
            copy(attn_wT[:], bank[2][:].rearrange("p (c d) -> p c d", c=4)).then_inc(consts_made, 1)

            def route(q):
                for j in range(QUADS):
                    act.wait_ge(xn_transposed, q * QUADS + j + 1)
                    copy(xnT[:, 512 * j:512 * j + 512], bank[j % 2][:]).then_inc(xnT_ready, 1)
                act.wait_ge(exp_asked, q + 1)
                act.activation(probs[:, :, 0:E], logits[:, :, 0:E], ACT.Exp).then_inc(exp_done, 1)
                for j in range(QUADS):
                    act.wait_ge(shared_h_done, q * QUADS + j + 1)
                    act.activation(sharedT[:, 512 * j:512 * j + 512], bank[2 + j % 2][:], ACT.Gelu,
                                   bias=bs1_col[:]).then_inc(sharedT_ready, 1)
                act.wait_ge(gates_transposed, q + 1)
                copy(gatesT[:].rearrange("p j t -> p (j t)"), bank[0][:]).then_inc(gatesT_ready, 1)

            def run_experts(q):
                def step(C, i, head, tail):
                    wait_chunks(act, h_done, C + 1, i)
                    wait_chunks(act, y_done, C - 1, i)
                    for u in range(CH):
                        ins = act.activation(hT[:, C % 2, u * P:(u + 1) * P], bank[2 + C % 2][:, u * P:(u + 1) * P],
                                             ACT.Gelu, bias=w_ring[:, C % RING, u, 2 * F:2 * F + 1])
                    ins.then_inc(hT_ready, 1)

                chunk_steps(act, q, step)

            def attend(g):
                first = g * GT

                def quad(j):
                    n = g * QUADS + j
                    act.wait_ge(xa_transposed, n + 1)
                    copy(xaT[:, n % 2, :], bank[0][:]).then_inc(xaT_ready, 1)

                def values(t):
                    act.wait_ge(qkv_done, t + 1)
                    act.wait_ge(qk_ready, t + 1)
                    if t >= 2:
                        act.wait_ge(kv_ready, t - 1)
                        act.wait_ge(state_done, t - 1)
                    copy(v_aug[:, t % 2, :, 0:HD],
                         bank[1][:, 2 * D:3 * D].rearrange("p (h e) -> p h e", h=HEADS)).then_inc(v_ready, 1)

                def transposed(n):
                    act.wait_ge(q_o_transposed, n + 1)
                    lo, hi = (0, 1) if n == g * (GT + 1) else (1, 2) if n == g * (GT + 1) + GT else (0, 2)
                    copy(q_oT[:, lo:hi, :], bank[7][:, lo * P:hi * P].rearrange("p (c t) -> p c t", t=P)
                         ).then_inc(q_oT_ready, 1)

                quad(0)
                for t in range(3):
                    values(first + t)
                    if t == 0:
                        transposed(g * (GT + 1))
                for t in range(GT):
                    if t % 4 == 0 and t + 4 < GT:
                        quad(t // 4 + 1)
                    if t > 0 and t + 2 < GT:
                        values(first + t + 2)
                    transposed(g * (GT + 1) + t + 1)

            for layer in range(2):
                if layer == 0:
                    route(0)
                    route(1)
                run_experts(2 * layer)
                run_experts(2 * layer + 1)
                if layer == 0:
                    for g in range(GROUPS):
                        attend(g)
                        route(GROUPS + g)

        @block.tensor
        def _(pe):
            pe.wait_ge(consts_made, 1)
            pe.wait_ge(attn_w_loaded, 16 * N_ATTN_W)
            pe.wait_ge(router_w_loaded, 16 * N_ROUTER_W)
            pe.transpose(bank[3][:, 0:E], be1_rows[:], ident[0:E, 0:E])
            for c in range(4):
                ins = pe.transpose(bank[2][:, c * P:(c + 1) * P], attn_rows[:, c, :], ident[:])
            ins.then_inc(w_transposed, 1)

            def route(q):
                g = q % GROUPS
                for j in range(QUADS):
                    pe.wait_ge(xn_ready, q * QUADS + j + 1)
                    if q * QUADS + j >= 2:
                        pe.wait_ge(xnT_ready, q * QUADS + j - 1)
                    for i in range(4):
                        ins = pe.transpose(bank[j % 2][:, i * P:(i + 1) * P], xn[:, g * GT + 4 * j + i, :], ident[:])
                    ins.then_inc(xn_transposed, 1)
                for t in range(GT):
                    if t % 4 == 0:
                        pe.wait_ge(xnT_ready, q * QUADS + t // 4 + 1)
                    ins = pe.matmul(bank[6][:, t * RP:t * RP + E], xnT[:, t * P:(t + 1) * P], wr_sb[:],
                                    start=True, stop=True)
                ins.then_inc(logits_done, 1)
                if q == 0:
                    pe.wait_ge(consts_made, 3)
                for j in range(QUADS):
                    if q * QUADS + j >= 2:
                        pe.wait_ge(sharedT_ready, q * QUADS + j - 1)
                    pe.matmul(bank[2 + j % 2][:], ws1_sb[:], xnT[:, 512 * j:512 * j + 512],
                              start=True, stop=True).then_inc(shared_h_done, 1)
                pe.wait_ge(chosen_ready, q + 1)
                pe.matmul(bank[7][:, 0:GT * E], before[:], chosen[:].rearrange("p t e -> p (t e)"),
                          start=True, stop=False, skip_group_check=True)
                for s in range(1, GT):
                    pe.matmul(bank[7][:, s * E:GT * E], ones[:], chosen[:, 0:GT - s, :].rearrange("p t e -> p (t e)"),
                              start=False, stop=s == GT - 1, skip_group_check=True)
                for t in range(GT):
                    ins = pe.matmul(bank[6][:, 0:E], ones[:], chosen[:, t, :], start=t == 0, stop=t == GT - 1)
                ins.then_inc(ranks_done, 1)
                pe.wait_ge(gates_ready, q + 1)
                for j in range(QUADS):
                    ins = pe.transpose(bank[0][:, j * P:(j + 1) * P],
                                       gates[:, 4 * j:4 * j + 4, :].rearrange("p t e -> p (t e)"), ident[:])
                ins.then_inc(gates_transposed, 1)
                pe.wait_ge(tile_expert_ready, q + 1)
                pe.matmul(bank[6][0:1, P:2 * P], tile_expert[:], ident[:], start=True, stop=True
                          ).then_inc(expert_row_done, 1)
                pe.wait_ge(gatesT_ready, q + 1)
                for j in range(QUADS):
                    pe.wait_ge(sharedT_ready, q * QUADS + j + 1)
                    if q * QUADS + j >= 2:
                        pe.wait_ge(shared_out_read, q * QUADS + j - 1)
                    for i in range(4):
                        o = bank[4 + j % 2][:, i * P:(i + 1) * P]
                        t = 4 * j + i
                        pe.matmul(o, sharedT[:, t * P:(t + 1) * P], ws2_sb[:], start=True, stop=False)
                        ins = pe.matmul(o, gatesT[:, j, :], be2_aug[:, i, :],
                                        start=False, stop=True)
                    ins.then_inc(shared_out_done, 1)

            def run_experts(q):
                pe.wait_ge(router_done, 2 * (q // 2 + 1))

                def transposes(C, i):
                    r = C % RING
                    pe.wait_ge(xs_loaded[r], 16 * (C // RING + 1) + (i * 16 if not isinstance(i, int) else 0))
                    wait_chunks(pe, xsT_ready, C - 1, i)
                    for u in range(CH):
                        ins = pe.transpose(bank[C % 2][:, u * P:(u + 1) * P], xs_in[:, r, u, :], ident[:])
                    ins.then_inc(xs_transposed, 1)

                def down(C, i):
                    wait_chunks(pe, hT_ready, C + 1, i)
                    wait_chunks(pe, ys_ready, C - 1, i)
                    for u in range(CH):
                        ins = pe.matmul(bank[4 + C % 2][:, u * P:(u + 1) * P], hT[:, C % 2, u * P:(u + 1) * P],
                                        w_ring[:, C % RING, u, F:2 * F], start=True, stop=True)
                    ins.then_inc(y_done, 1)

                def step(C, i, head, tail):
                    if head:
                        transposes(C, i)
                    if not tail:
                        transposes(C + 1, i)
                    wait_chunks(pe, xsT_ready, C + 1, i)
                    wait_chunks(pe, weights_copied, C + 1, i)
                    wait_chunks(pe, hT_ready, C - 1, i)
                    for u in range(CH):
                        ins = pe.matmul(bank[2 + C % 2][:, u * P:(u + 1) * P], w_ring[:, C % RING, u, 0:F],
                                        xsT[:, C % 2, u * P:(u + 1) * P], start=True, stop=True)
                    ins.then_inc(h_done, 1)
                    if not head:
                        down(C - 1, i)
                    if tail:
                        down(C, i)

                chunk_steps(pe, q, step)

            def attend(g):
                first = g * GT
                burst0 = g * (GT + 1)

                def quad(j):
                    n = g * QUADS + j
                    pe.wait_ge(xa_ready, n + 1)
                    if n >= 1:
                        pe.wait_ge(xaT_ready, n)
                    for i in range(4):
                        ins = pe.transpose(bank[0][:, i * P:(i + 1) * P], xa[:, i, :], ident[:])
                    ins.then_inc(xa_transposed, 1)

                def project(t):
                    n = first + t
                    if t % 4 == 0:
                        pe.wait_ge(xaT_ready, n // 4 + 1)
                    if n >= 1:
                        pe.wait_ge(qk_ready, n)
                        pe.wait_ge(v_ready, n)
                    o = bank[1][:, 0:3 * D]
                    pe.matmul(o, xaT[:, (n // 4) % 2, (t % 4) * P:(t % 4 + 1) * P],
                              attn_wT[:, 0:3, :].rearrange("p c d -> p (c d)"), start=True, stop=False)
                    pe.matmul(o, ones_row[:], qkv_bias[:], start=False, stop=True).then_inc(qkv_done, 1)

                def running_sums(t):
                    n = first + t
                    pe.wait_ge(kv_ready, n + 1)
                    if n >= 1:
                        pe.wait_ge(sums_read, n)
                    for c, (a, b) in enumerate(HEAD_CUTS):
                        ins = pe.matmul(bank[2 + c][:, 0:(b - a) * HA * HD], tri[:],
                                        kv[:, n % 2, a:b, :, :].rearrange("p h e d -> p (h e d)"),
                                        start=True, stop=True)
                    ins.then_inc(sums_done, 1)
                    if n >= 1:
                        pe.wait_ge(state_ready, n)
                    pe.matmul(bank[5][:, 0:HEADS * HA], qk[:, n % 2, D:2 * D],
                              v_aug[:, n % 2, :, :].rearrange("p h e -> p (h e)"), start=t % BT == 0,
                              stop=True, skip_group_check=True).then_inc(state_done, 1)

                def burst(t):
                    n = burst0 + t
                    if t > 0:
                        pe.wait_ge(attn_o_ready, first + t)
                    if n >= 1:
                        pe.wait_ge(q_oT_ready, n)
                    if t < GT:
                        pe.wait_ge(qk_ready, first + t + 1)
                        ins = pe.transpose(bank[7][:, 0:P], qk[:, (first + t) % 2, 0:D], ident[:])
                    if t > 0:
                        ins = pe.transpose(bank[7][:, P:2 * P], attn_o[:], ident[:])
                    ins.then_inc(q_o_transposed, 1)
                    pe.wait_ge(q_oT_ready, n + 1)
                    if n >= 1:
                        pe.wait_ge(in_out_read, n)
                    if t % BT and t < GT:
                        pe.wait_ge(state_ready, first + t)
                        ins = pe.matmul(bank[6][:, 0:HEADS * HA], q_oT[:, 0, :], state[:], start=True, stop=True)
                    if t > 0:
                        o = bank[6][:, 2 * P:3 * P]
                        pe.matmul(o, q_oT[:, 1, :], attn_wT[:, 3, :], start=True, stop=False)
                        ins = pe.matmul(o, ones_row[:], out_bias[:], start=False, stop=True)
                    if t > 0:
                        ins.then_inc(in_out_done, 1)
                    else:
                        pe.nop().then_inc(in_out_done, 1)

                quad(0)
                project(0)
                burst(0)
                project(1)
                running_sums(0)
                project(2)
                for t in range(GT):
                    if t + 1 < GT:
                        running_sums(t + 1)
                    if t % 4 == 0 and t + 4 < GT:
                        quad(t // 4 + 1)
                    burst(t + 1)
                    if t + 3 < GT:
                        project(t + 3)

            for layer in range(2):
                if layer == 0:
                    route(0)
                    route(1)
                run_experts(2 * layer)
                run_experts(2 * layer + 1)
                if layer == 0:
                    for g in range(GROUPS):
                        attend(g)
                        route(GROUPS + g)

        @block.vector
        def _(dve):
            steps = [0]

            def link(ins):
                steps[0] += 1
                ins.then_inc(dve_step, 1)
                dve.wait_ge(dve_step, steps[0])

            def norm_stats(first, n):
                m, v, r, a, b = (s[:, 0:n] for s in (mean, var, rstd, tmp_a, tmp_b))
                for t in range(n):
                    ins = dve.bn_stats(stats[:, t, :], x[:, first + t, :])
                link(ins)
                s = stats[:, 0:n, :]
                dve.tensor_tensor(a, s[:, :, 1], s[:, :, 4], ALU.subtract)
                dve.tensor_tensor(b, s[:, :, 2], s[:, :, 5], ALU.add)
                link(dve.tensor_tensor(r, s[:, :, 1], s[:, :, 4], ALU.add))
                dve.tensor_scalar(m, r, 0.5, None, ALU.mult)
                dve.tensor_scalar(b, b, 1.0 / D, LN_EPS, ALU.mult, ALU.add)
                link(dve.scalar_tensor_tensor(out=v, in0=a, scalar=0.25, in1=a, op0=ALU.mult, op1=ALU.mult))
                link(dve.tensor_tensor(v, v, b, ALU.add))
                link(dve.tensor_scalar(seed[:, 0:n], v.bitcast(I32), 1, None, ALU.logical_shift_right))
                link(dve.tensor_copy(seed_f[:, 0:n], seed[:, 0:n]))
                link(dve.tensor_scalar(seed[:, 0:n], seed_f[:, 0:n], -1.0, float(RSQRT_SEED), ALU.mult, ALU.add))
                y = seed[:, 0:n].bitcast(F32)
                for k in range(4):
                    link(dve.tensor_tensor(a, y, y, ALU.mult))
                    link(dve.scalar_tensor_tensor(out=b, in0=a, scalar=-0.5, in1=v, op0=ALU.mult, op1=ALU.mult))
                    link(dve.scalar_tensor_tensor(out=r, in0=b, scalar=1.5, in1=y, op0=ALU.add, op1=ALU.mult))
                    y = r

            def over_tiles(a):
                return a.unsqueeze(1).broadcast_to([P, GT, E])

            def route(q):
                g = q % GROUPS
                first = g * GT
                if q < GROUPS:
                    dve.wait_ge(x_loaded[g], 16)
                norm_stats(first, GT)
                if q >= GROUPS:
                    dve.wait_ge(xs_scattered[g], 16 * GT * TOPK * (q // GROUPS))
                for t in range(GT):
                    ins = dve.tensor_scalar(xn[:, first + t, :], x[:, first + t, :], mean[:, t:t + 1],
                                            rstd[:, t:t + 1], ALU.subtract, ALU.mult)
                    if t % 4 == 3:
                        ins.then_inc(xn_ready, 1)
                dve.wait_ge(xn_ready, QUADS * (q + 1))
                xg = x[:, first:first + GT, :]
                link(dve.scalar_tensor_tensor(out=xg, in0=xn[:, first:first + GT, :], scalar=0.5, in1=xg,
                                              op0=ALU.mult, op1=ALU.add))
                if q == 0:
                    dve.wait_ge(w_transposed, 1)
                    dve.tensor_copy(experts[:, :, 2 * F], bank[3][:, 0:E]).then_inc(consts_made, 1)
                    dve.wait_ge(router_w_loaded, 16 * N_ROUTER_W)
                lg, pr = logits[:, :, 0:E], probs[:, :, 0:E]
                dve.wait_ge(logits_done, q + 1)
                link(dve.tensor_tensor(lg, bank[6][:].rearrange("p (t e) -> p t e", e=RP)[:, :, 0:E],
                                       over_tiles(br_all[:]), ALU.add))
                link(dve.tensor_reduce(row_max[:], lg, AXX, ALU.max))
                dve.tensor_tensor(lg, lg, row_max[:].unsqueeze(2).broadcast_to([P, GT, E]), ALU.subtract
                                  ).then_inc(exp_asked, 1)
                dve.wait_ge(exp_done, q + 1)
                link(dve.tensor_reduce(row_sum[:], pr, AXX, ALU.add))
                link(dve.reciprocal(row_sum[:], row_sum[:]))
                link(dve.tensor_tensor(pr, pr, row_sum[:].unsqueeze(2).broadcast_to([P, GT, E]), ALU.mult))
                for t in range(GT):
                    ins = dve.max(top[:, t, :], probs[:, t, 0:E])
                link(ins)
                for t in range(GT):
                    ins = dve.max_index(top_id[:, t, :], top[:, t, :], probs[:, t, 0:E])
                link(dve.tensor_scalar(half_gate[:, first:first + GT, :], top[:, :, 0:TOPK], 0.5, None, ALU.mult))
                link(dve.tensor_copy(top_idf[:], top_id[:, :, 0:TOPK]))
                link(dve.tensor_tensor(one_hot[:], top_idf[:].unsqueeze(3).broadcast_to([P, GT, TOPK, E]),
                                       expert_ids[:].unsqueeze(1).unsqueeze(1).broadcast_to([P, GT, TOPK, E]),
                                       ALU.is_equal))
                link(dve.tensor_tensor(chosen_a[:], one_hot[:, :, 0, :], one_hot[:, :, 1, :], ALU.add))
                dve.tensor_tensor(chosen[:], chosen_a[:], one_hot[:, :, 2, :], ALU.add).then_inc(chosen_ready, 1)
                dve.wait_ge(chosen_ready, q + 1)
                dve.tensor_tensor(gates[:, :, 0:E], pr, chosen[:], ALU.mult).then_inc(gates_ready, 1)
                dve.wait_ge(ranks_done, q + 1)
                link(dve.tensor_scalar(count_i[:], bank[6][:, 0:E], float(P - 1), None, ALU.add))
                link(dve.tensor_scalar(count_t[:], count_i[:], 7, None, ALU.logical_shift_right))
                link(dve.tensor_copy(run_tiles[:], count_t[:]))
                link(dve.tensor_tensor_scan(run_end[:], run_tiles[:], zero_row[:], 0.0, ALU.add, ALU.add))
                dve.tensor_scalar(ended[:], run_end[:], row_id[:, 0:1], None, ALU.is_le)
                link(dve.tensor_tensor(run_base[:], run_end[:], run_tiles[:], ALU.subtract))
                link(dve.tensor_reduce(tile_expert[:], ended[:], AXX, ALU.add))
                dve.tensor_scalar(tile_expert[:], tile_expert[:], float(E - 1), None, ALU.min
                                  ).then_inc(tile_expert_ready, 1)
                link(dve.tensor_scalar(run_base[:], run_base[:], float(P), None, ALU.mult))
                link(dve.tensor_tensor(slot_of[:], bank[7][:, 0:GT * E].rearrange("p (t e) -> p t e", e=E),
                                       over_tiles(run_base[:]), ALU.add))
                link(dve.tensor_tensor(hot_slots[:], one_hot[:],
                                       slot_of[:].unsqueeze(2).broadcast_to([P, GT, TOPK, E]), ALU.mult))
                link(dve.tensor_reduce(slot_f[:], hot_slots[:], AXX, ALU.add))
                dve.tensor_copy(slots[:, first:first + GT, :], slot_f[:]).then_inc(slots_ready, 1)
                dve.wait_ge(expert_row_done, q + 1)
                link(dve.tensor_copy(expert_tab[0:1, g * P:g * P + P], bank[6][0:1, P:2 * P]))
                for j in range(QUADS):
                    dve.wait_ge(shared_out_done, q * QUADS + j + 1)
                    xq = x[:, first + 4 * j:first + 4 * j + 4, :].rearrange("p t d -> p (t d)")
                    dve.scalar_tensor_tensor(out=xq, in0=bank[4 + j % 2][:], scalar=0.5, in1=xq,
                                             op0=ALU.mult, op1=ALU.add).then_inc(shared_out_read, 1)
                dve.wait_ge(shared_out_read, QUADS * (q + 1))
                dve.tensor_copy(tmp_b[:], row_max[:]).then_inc(router_done, 1)
                dve.wait_ge(router_done, q + 1)

            def run_experts(q):
                g = q % GROUPS

                def weights(C, i):
                    wait_chunks(dve, y_done, C - RING + 1, i)
                    for u in range(CH):
                        at = g * P + (C - q * CHUNKS) * CH + u
                        at = slice(at, at + 1) if isinstance(i, int) else bass.ds(i * (RING * CH) + at, 1)
                        e = dve.value_load(expert_tab[0:1, at], min_val=0, max_val=E - 1)
                        ins = dve.tensor_copy(w_ring[:, C % RING, u:u + 1, :], experts[:, bass.ds(e, 1), :])
                    ins.then_inc(weights_copied, 1)

                def turned(C, i):
                    wait_chunks(dve, xs_transposed, C + 1, i)
                    wait_chunks(dve, h_done, C - 1, i)
                    dve.tensor_copy(xsT[:, C % 2, :], bank[C % 2][:, 0:CH * P]).then_inc(xsT_ready, 1)

                def results(C, i):
                    wait_chunks(dve, y_done, C + 1, i)
                    if C >= RING:
                        dve.wait_ge(ys_stored[C % RING], 16 * (C // RING) + (i * 16 if not isinstance(i, int) else 0))
                    elif not isinstance(i, int):
                        dve.wait_ge(ys_stored[C % RING], i * 16)
                    dve.tensor_copy(ys_out[:, C % RING, :, :].rearrange("p u d -> p (u d)"),
                                    bank[4 + C % 2][:, 0:CH * P]).then_inc(ys_ready, 1)

                def step(C, i, head, tail):
                    if head:
                        weights(C, i)
                        turned(C, i)
                    if not tail:
                        weights(C + 1, i)
                        turned(C + 1, i)
                    c = C - q * CHUNKS
                    if c >= 2:
                        results(C - 2, i)
                    if tail:
                        results(C - 1, i)
                        results(C, i)

                if q == 0:
                    dve.wait_ge(experts_loaded, 32)
                chunk_steps(dve, q, step)

            def combine(q, j):
                n = q * QUADS + j
                dve.wait_ge(y_gathered[n % 2], 16 * 4 * TOPK * (n // 2 + 1))
                first = (q % GROUPS) * GT + 4 * j
                for k in range(TOPK):
                    for t in range(first, first + 4):
                        ins = dve.scalar_tensor_tensor(out=x[:, t, :], in0=y_tok[:, t, k, :],
                                                       scalar=half_gate[:, t, k:k + 1], in1=x[:, t, :],
                                                       op0=ALU.mult, op1=ALU.add)
                    if k < TOPK - 1 or q < GROUPS:
                        link(ins)
                return ins

            def attend(g):
                first = g * GT
                burst0 = g * (GT + 1)

                def quad(j):
                    n = g * QUADS + j
                    combine(g, j)
                    norm_stats(first + 4 * j, 4)
                    if n >= 1:
                        dve.wait_ge(xa_transposed, n)
                    for i in range(4):
                        ins = dve.tensor_scalar(xa[:, i, :], x[:, first + 4 * j + i, :], mean[:, i:i + 1],
                                                rstd[:, i:i + 1], ALU.subtract, ALU.mult)
                    ins.then_inc(xa_ready, 1)

                def features(t):
                    n = first + t
                    dve.wait_ge(qkv_done, n + 1)
                    dve.tensor_scalar(qk[:, n % 2, :], bank[1][:, 0:2 * D], 0.0, FEATURE_EPS, ALU.max, ALU.add
                                      ).then_inc(qk_ready, 1)

                def outer(t):
                    n = first + t
                    dve.wait_ge(v_ready, n + 1)
                    dve.wait_ge(qk_ready, n + 1)
                    if n >= 2:
                        dve.wait_ge(sums_done, n - 1)
                    k = qk[:, n % 2, D:2 * D].rearrange("p (h d) -> p h d", h=HEADS)
                    dve.tensor_tensor(kv[:, n % 2, :, :, :], k.unsqueeze(2).broadcast_to([P, HEADS, HA, HD]),
                                      v_aug[:, n % 2, :, :].unsqueeze(3).broadcast_to([P, HEADS, HA, HD]), ALU.mult
                                      ).then_inc(kv_ready, 1)

                def apply(t):
                    n = first + t
                    dve.wait_ge(sums_done, n + 1)
                    qh = qk[:, n % 2, 0:D].rearrange("p (h d) -> p h d", h=HEADS)
                    for c, (a, b) in enumerate(HEAD_CUTS):
                        s = bank[2 + c][:, 0:(b - a) * HA * HD].rearrange("p (h e d) -> p h e d", e=HA, d=HD)
                        ins = dve.tensor_tensor(weighed[:, a:b, :, :], s,
                                                qh[:, a:b, :].unsqueeze(2).broadcast_to([P, b - a, HA, HD]), ALU.mult)
                    ins.then_inc(sums_read, 1)
                    dve.wait_ge(sums_read, n + 1)
                    link(dve.tensor_reduce(num_den[:], weighed[:], AXX, ALU.add))
                    dve.wait_ge(in_out_done, burst0 + t + 1)
                    if t % BT:
                        nd = num_den[:].rearrange("p h e -> p (h e)")
                        link(dve.tensor_tensor(nd, nd, bank[6][:, 0:HEADS * HA], ALU.add))
                    project_out(t)
                    link(dve.tensor_scalar(den[:], num_den[:, :, HD], DEN_EPS, None, ALU.max))
                    link(dve.reciprocal(den_inv[:], den[:]))
                    dve.tensor_tensor(attn_o[:].rearrange("p (h e) -> p h e", h=HEADS), num_den[:, :, 0:HD],
                                      den_inv[:].unsqueeze(2).broadcast_to([P, HEADS, HD]), ALU.mult
                                      ).then_inc(attn_o_ready, 1)
                    dve.wait_ge(attn_o_ready, n + 1)
                    dve.wait_ge(state_done, n + 1)
                    dve.tensor_tensor(state[:], bank[5][:, 0:HEADS * HA],
                                      head_mask[:].rearrange("p h e -> p (h e)"), ALU.mult).then_inc(state_ready, 1)
                    dve.wait_ge(state_ready, n + 1)

                def project_out(t):
                    if t > 0:
                        xt = x[:, first + t - 1, :]
                        ins = dve.tensor_tensor(xt, xt, bank[6][:, 2 * P:3 * P], ALU.add)
                    else:
                        ins = dve.tensor_copy(tmp_a[:, 0:1], tmp_b[:, 0:1])
                    ins.then_inc(in_out_read, 1)
                    dve.wait_ge(in_out_read, burst0 + t + 1)

                quad(0)
                features(0)
                outer(0)
                features(1)
                for t in range(GT):
                    if t + 1 < GT:
                        outer(t + 1)
                    apply(t)
                    if t + 2 < GT:
                        features(t + 2)
                    if t % 4 == 0 and t + 4 < GT:
                        quad(t // 4 + 1)
                dve.wait_ge(in_out_done, burst0 + GT + 1)
                project_out(GT)

            for layer in range(2):
                if layer == 0:
                    route(0)
                    route(1)
                run_experts(2 * layer)
                run_experts(2 * layer + 1)
                for g in range(GROUPS):
                    if layer == 0:
                        attend(g)
                        route(GROUPS + g)
                    else:
                        for j in range(QUADS):
                            combine(GROUPS + g, j).then_inc(x_final, 1)


_INS = ['L0_attn_x', 'L0_attn_qkv_w', 'L0_attn_qkv_b', 'L0_attn_out_w', 'L0_attn_out_b',
        'L0_ffn_ws1', 'L0_ffn_bs1', 'L0_ffn_ws2', 'L0_ffn_bs2', 'L0_ffn_We1', 'L0_ffn_Be1',
        'L0_ffn_We2', 'L0_ffn_Be2', 'L0_ffn_Wr', 'L0_ffn_br']


def kernel(**inputs):
    import numpy as _np
    import concourse.bacc as _bacc
    from concourse import mybir as _mybir
    from concourse.bass_utils import run_bass_kernel_spmd as _run

    nc = _bacc.Bacc("TRN2", target_bir_lowering=False, num_devices=1)
    arrays, args = {}, []
    for name in _INS:
        a = _np.ascontiguousarray(inputs[name])
        arrays[f"in_{name}_dram"] = a
        args.append(nc.dram_tensor(f"in_{name}_dram", a.shape, _mybir.dt.from_np(a.dtype), kind="ExternalInput").ap())
    shape = inputs['L0_attn_x'].shape
    args.append(nc.dram_tensor("out_0_dram", shape, _mybir.dt.float32, kind="ExternalOutput").ap())
    macaron_kernel(nc, *args)
    r = _run(nc, [arrays], core_ids=[0])
    return r.results[0]["out_0_dram"]
```

```python
from contextlib import ExitStack

import concourse.bass as bass
from concourse import mybir

F32 = mybir.dt.float32
BF16 = mybir.dt.bfloat16
I32 = mybir.dt.int32
U32 = mybir.dt.uint32
ALU = mybir.AluOpType
ACT = mybir.ActivationFunctionType
AXX = mybir.AxisListType.X

P = 128
LN_EPS = 1e-5
FEATURE_EPS = 1e-6
DEN_EPS = 1e-6
RSQRT_SEED = 0x5F3759DF


def macaron_kernel(nc, x_in, qkv_w, qkv_b, out_w, out_b, ws1, bs1, ws2, bs2,
                   we1, be1, we2, be2, wr, br, out):
    BATCH, SEQ, D = x_in.shape
    E, _, F = we1.shape
    TOPK = 3
    HEADS, HD = 16, D // 16
    HA = HD + 1
    TILES = BATCH * SEQ // P
    GROUPS = 2
    GT = TILES // GROUPS
    BT = SEQ // P
    QUADS = GT // 4
    PAIRS = GT * P * TOPK
    SLOT_TILES = PAIRS // P - 1 + E
    CH = 3
    CHUNKS = SLOT_TILES // CH
    RING = 4
    RP = 32
    W_COLS = 2 * F + 1
    assert D == P and F == P and SLOT_TILES % CH == 0 and (CHUNKS - 2) % RING == 0
    HEAD_CUTS = [(0, 6), (6, 11), (11, 16)]

    x_tok = x_in.rearrange("b (t p) d -> p (b t) d", p=P)
    out_tok = out.rearrange("b (t p) d -> p (b t) d", p=P)
    def scratch(name):
        rows = [nc.dram_tensor(f"{name}{g}", [SLOT_TILES * P, D], F32, kind="Internal").ap() for g in range(GROUPS)]
        return rows, [r.rearrange("(c u p) d -> p c u d", u=CH, p=P) for r in rows]

    xs_rows, xs_chunks = scratch("xs_rows")
    ys_rows, ys_chunks = scratch("ys_rows")

    with ExitStack() as ctx:
        def sb(name, shape, dt=F32):
            return ctx.enter_context(nc.sbuf_tensor(name, shape, dt))

        def sem(name):
            return ctx.enter_context(nc.semaphore(name))

        bank = [ctx.enter_context(nc.psum_tensor(f"bank{i}", [P, 512], F32)) for i in range(8)]

        experts = sb("experts", [P, E, W_COLS])
        be1_rows = sb("be1_rows", [E, F])
        be2_aug = sb("be2_aug", [P, 4, D])
        wr_sb = sb("wr_sb", [P, E])
        br_all = sb("br_all", [P, E])
        ws1_sb = sb("ws1_sb", [P, F])
        ws2_sb = sb("ws2_sb", [P, D])
        bs1_col = sb("bs1_col", [P, 1])
        attn_rows = sb("attn_rows", [P, 4, D])
        attn_wT = sb("attn_wT", [P, 4, D])
        qkv_bias = sb("qkv_bias", [1, 3 * D])
        out_bias = sb("out_bias", [1, D])
        ident = sb("ident", [P, P])
        tri = sb("tri", [P, P])
        ones_row = sb("ones_row", [1, P])
        before = sb("before", [P, P], BF16)
        ones = sb("ones", [P, P], BF16)
        head_mask = sb("head_mask", [P, HEADS, HA])
        expert_ids = sb("expert_ids", [P, E])
        row_id = sb("row_id", [P, 1])

        x = sb("x", [P, TILES, D])
        xn = sb("xn", [P, TILES, D])
        xnT = sb("xnT", [P, GT * P])
        sharedT = sb("sharedT", [P, GT * P])
        stats = sb("stats", [P, GT, 6])
        mean = sb("mean", [P, GT])
        var = sb("var", [P, GT])
        rstd = sb("rstd", [P, GT])
        tmp_a = sb("tmp_a", [P, GT])
        tmp_b = sb("tmp_b", [P, GT])
        rstd4 = sb("rstd4", [P, 4])
        shift4 = sb("shift4", [P, 4])
        shift = sb("shift", [P, GT])
        seed = sb("seed", [P, GT], I32)
        seed_f = sb("seed_f", [P, GT])
        logits = sb("logits", [P, GT, RP])
        probs = sb("probs", [P, GT, RP])
        row_max = sb("row_max", [P, GT])
        row_sum = sb("row_sum", [P, GT])
        top = sb("top", [P, GT, 8])
        top_id = sb("top_id", [P, GT, 8], U32)
        top_idf = sb("top_idf", [P, GT, TOPK])
        one_hot = sb("one_hot", [P, GT, TOPK, E])
        hot_slots = sb("hot_slots", [P, GT, TOPK, E])
        chosen_a = sb("chosen_a", [P, GT, E])
        chosen = sb("chosen", [P, GT, E], BF16)
        gates = sb("gates", [P, GT, RP])
        gatesT = sb("gatesT", [P, QUADS, P])
        half_gate = sb("half_gate", [P, TILES, TOPK])
        count_i = sb("count_i", [P, E], I32)
        count_t = sb("count_t", [P, E], I32)
        run_tiles = sb("run_tiles", [P, E])
        run_end = sb("run_end", [P, E])
        run_base = sb("run_base", [P, E])
        zero_row = sb("zero_row", [P, E])
        slot_of = sb("slot_of", [P, GT, E])
        slot_f = sb("slot_f", [P, GT, TOPK])
        slots = sb("slots", [P, TILES, TOPK], U32)
        ended = sb("ended", [P, E])
        tile_expert = sb("tile_expert", [P, 1])
        expert_tab = sb("expert_tab", [1, GROUPS * P], I32)
        y_tok = sb("y_tok", [P, TILES, TOPK, D])

        xs_in = sb("xs_in", [P, RING, CH, D])
        xsT = sb("xsT", [P, 2, CH * P])
        w_ring = sb("w_ring", [P, RING, CH, W_COLS])
        hT = sb("hT", [P, 2, CH * P])
        ys_out = sb("ys_out", [P, RING, CH, D])

        zeros = ys_out[:, 0, 0, :]

        xaT = sharedT[:, 0:2 * 4 * P].rearrange("p (b n) -> p b n", b=2)
        xa = sharedT[:, 2 * 4 * P:3 * 4 * P].rearrange("p (t d) -> p t d", d=D)
        qk_relu = sb("qk_relu", [P, 2 * D])
        qk = sb("qk", [P, 2, 2 * D])
        v_aug = sb("v_aug", [P, 2, HEADS, HA])
        kv = w_ring[:].rearrange("p r u w -> p (r u w)")[:, 0:2 * HEADS * HA * HD].rearrange(
            "p (b h e d) -> p b h e d", b=2, e=HA, d=HD)
        weighed = hot_slots[:].rearrange("p t k e -> p (t k e)")[:, 0:HEADS * HA * HD].rearrange(
            "p (h e d) -> p h e d", e=HA, d=HD)
        num_den = sb("num_den", [P, HEADS, HA])
        den = sb("den", [P, HEADS])
        den_inv = sb("den_inv", [P, HEADS])
        attn_o = sb("attn_o", [P, D])
        q_oT = sb("q_oT", [P, 2, P])
        state = sb("state", [P, HEADS * HA])

        x_loaded = [sem(f"x_loaded{g}") for g in range(GROUPS)]
        router_w_loaded = sem("router_w_loaded")
        attn_w_loaded = sem("attn_w_loaded")
        experts_loaded = sem("experts_loaded")
        zeros_made = sem("zeros_made")
        slots_zeroed = [sem(f"slots_zeroed{g}") for g in range(GROUPS)]
        consts_made = sem("consts_made")
        pool_step = sem("pool_step")
        dve_step = sem("dve_step")
        w_transposed = sem("w_transposed")
        xn_ready = sem("xn_ready")
        xn_transposed = sem("xn_transposed")
        xnT_ready = sem("xnT_ready")
        logits_done = sem("logits_done")
        exp_asked = sem("exp_asked")
        exp_done = sem("exp_done")
        chosen_ready = sem("chosen_ready")
        gates_ready = sem("gates_ready")
        ranks_done = sem("ranks_done")
        slots_ready = sem("slots_ready")
        tile_expert_ready = sem("tile_expert_ready")
        expert_row_done = sem("expert_row_done")
        shared_h_done = sem("shared_h_done")
        sharedT_ready = sem("sharedT_ready")
        gates_transposed = sem("gates_transposed")
        gatesT_ready = sem("gatesT_ready")
        shared_out_done = sem("shared_out_done")
        shared_out_read = sem("shared_out_read")
        router_done = sem("router_done")
        xs_scattered = [sem(f"xs_scattered{g}") for g in range(GROUPS)]
        xs_loaded = [sem(f"xs_loaded{r}") for r in range(RING)]
        xs_transposed = sem("xs_transposed")
        xsT_ready = sem("xsT_ready")
        weights_copied = sem("weights_copied")
        h_done = sem("h_done")
        hT_ready = sem("hT_ready")
        y_done = sem("y_done")
        ys_ready = sem("ys_ready")
        ys_stored = [sem(f"ys_stored{r}") for r in range(RING)]
        y_gathered = [sem(f"y_gathered{r}") for r in range(2)]
        norm_ready = sem("norm_ready")
        xa_ready = sem("xa_ready")
        xa_transposed = sem("xa_transposed")
        xaT_ready = sem("xaT_ready")
        qkv_done = sem("qkv_done")
        relu_done = sem("relu_done")
        features_ready = sem("features_ready")
        kv_ready = sem("kv_ready")
        sums_done = sem("sums_done")
        sums_read = sem("sums_read")
        state_done = sem("state_done")
        state_ready = sem("state_ready")
        attn_o_ready = sem("attn_o_ready")
        q_o_transposed = sem("q_o_transposed")
        q_oT_ready = sem("q_oT_ready")
        carried_done = sem("carried_done")
        carried_read = sem("carried_read")
        projected = sem("projected")
        x_attended = sem("x_attended")
        x_final = sem("x_final")
        out_stored = sem("out_stored")

        N_ROUTER_W = 6 + 8
        N_ATTN_W = 4
        N_EXPERT_W = 3

        def stored_before(c):
            return [(c - r + RING - 1) // RING for r in range(RING)]

        def chunk_steps(eng, q, step):
            first = q * CHUNKS
            for c in range(2):
                step(first + c, 0, c == 0, False)
            loops = (CHUNKS - 2) // RING - 1
            with eng.Fori(0, loops) as i:
                for c in range(RING):
                    step(first + 2 + c, i, False, False)
            for c in range(2 + RING * loops, CHUNKS):
                step(first + c, 0, False, c == CHUNKS - 1)

        def of_chunk(chunks, c, i):
            if isinstance(i, int):
                return chunks[:, c + RING * i, :, :]
            return chunks[:, bass.ds(i * RING + c, 1), :, :].rearrange("p c u d -> p (c u) d")

        def wait_chunks(eng, semaphore, n, i, each=1):
            if isinstance(i, int):
                if n + RING * i > 0:
                    eng.wait_ge(semaphore, each * (n + RING * i))
            else:
                eng.wait_ge(semaphore, i * (RING * each) + each * n)

        block = ctx.enter_context(nc.Block())

        @block.sync
        def _(sp):
            def load(dst, src, done):
                sp.dma_start(dst, src).then_inc(done, 16)

            def zero_slots(g):
                sp.dma_start(xs_rows[g].rearrange("(t p) d -> p t d", p=P),
                             zeros.unsqueeze(1).broadcast_to([P, SLOT_TILES, D])).then_inc(slots_zeroed[g], 16)

            load(x[:, 0:GT, :], x_tok[:, 0:GT, :], x_loaded[0])
            load(wr_sb[:], wr, router_w_loaded)
            load(br_all[:], br.unsqueeze(0).broadcast_to([P, E]), router_w_loaded)
            load(ws1_sb[:], ws1, router_w_loaded)
            load(ws2_sb[:], ws2, router_w_loaded)
            load(bs1_col[:], bs1.unsqueeze(1), router_w_loaded)
            load(be1_rows[:], be1, router_w_loaded)
            load(attn_rows[:, 0:3, :], qkv_w.rearrange("(c p) d -> p c d", p=P), attn_w_loaded)
            load(attn_rows[:, 3, :], out_w, attn_w_loaded)
            load(qkv_bias[:], qkv_b.unsqueeze(0), attn_w_loaded)
            load(out_bias[:], out_b.unsqueeze(0), attn_w_loaded)
            sp.wait_ge(zeros_made, 2)
            for j in range(4):
                load(be2_aug[RP * j:RP * j + E, j, :], be2, router_w_loaded)
                load(be2_aug[RP * j + E:RP * j + RP, j, :], bs2.unsqueeze(0), router_w_loaded)
            load(x[:, GT:2 * GT, :], x_tok[:, GT:2 * GT, :], x_loaded[1])
            zero_slots(0)
            load(experts[:, :, 0:F], we1.rearrange("e d f -> d e f"), experts_loaded)
            load(experts[:, :, F:2 * F], we2.rearrange("e f d -> f e d"), experts_loaded)
            zero_slots(1)

            def load_slots(q):
                g = q % GROUPS
                sp.wait_ge(xs_scattered[g], 16 * GT * TOPK * (q // GROUPS + 1))

                def load_chunk(C, i):
                    wait_chunks(sp, xs_transposed, C - RING + 1, i)
                    sp.dma_start(xs_in[:, C % RING, :, :], of_chunk(xs_chunks[g], C - q * CHUNKS, i)
                                 ).then_inc(xs_loaded[C % RING], 16)

                def step(C, i, head, tail):
                    if head:
                        load_chunk(C, i)
                        load_chunk(C + 1, i)
                    if C + 2 < (q + 1) * CHUNKS:
                        load_chunk(C + 2, i)

                chunk_steps(sp, q, step)

            for q in range(2 * GROUPS):
                load_slots(q)
            for j in range(TILES // 4):
                sp.wait_ge(x_final, j + 1)
                sp.dma_start(out_tok[:, 4 * j:4 * j + 4, :], x[:, 4 * j:4 * j + 4, :]).then_inc(out_stored, 16)
            sp.wait_ge(out_stored, 16 * (TILES // 4))

        @block.gpsimd
        def _(pool):
            pool.memset(be2_aug[:], 0.0).then_inc(zeros_made, 1)
            pool.memset(zeros, 0.0).then_inc(zeros_made, 1)
            made = [0]

            def link(ins):
                made[0] += 1
                ins.then_inc(pool_step, 1)
                pool.wait_ge(pool_step, made[0])

            pool.memset(ident[:], 0.0)
            pool.memset(tri[:], 1.0)
            pool.memset(before[:], 1.0)
            pool.memset(ones[:], 1.0)
            pool.memset(ones_row[:], 1.0)
            pool.memset(head_mask[:], 1.0)
            pool.memset(zero_row[:], 0.0)
            pool.memset(v_aug[:], 1.0)
            pool.memset(gates[:], 1.0)
            pool.iota(expert_ids[:], [[1, E]], base=0, channel_multiplier=0, allow_small_or_imprecise_dtypes=True)
            link(pool.iota(row_id[:], [[1, 1]], base=0, channel_multiplier=1, allow_small_or_imprecise_dtypes=True))
            pool.affine_select(out=ident[:], in_=ident[:], compare_op=ALU.not_equal, fill=1.0, base=0,
                               pattern=[[-1, P]], channel_multiplier=1)
            pool.affine_select(out=tri[:], in_=tri[:], compare_op=ALU.is_ge, fill=0.0, base=0,
                               pattern=[[1, P]], channel_multiplier=-1)
            pool.affine_select(out=before[:], in_=before[:], compare_op=ALU.is_ge, fill=0.0, base=-1,
                               pattern=[[1, P]], channel_multiplier=-1)
            link(pool.affine_select(out=head_mask[:], in_=head_mask[:], compare_op=ALU.is_ge, fill=0.0, base=0,
                                    pattern=[[-HD, HEADS], [0, HA]], channel_multiplier=1))
            pool.affine_select(out=head_mask[:], in_=head_mask[:], compare_op=ALU.is_ge, fill=0.0, base=HD - 1,
                               pattern=[[HD, HEADS], [0, HA]], channel_multiplier=-1).then_inc(consts_made, 1)

            def scatter(q):
                g = q % GROUPS
                pool.wait_ge(slots_zeroed[g], 16)
                pool.wait_ge(slots_ready, q + 1)
                for t in range(g * GT, (g + 1) * GT):
                    for k in range(TOPK):
                        pool.indirect_dma_start(xs_rows[g], bass.IndirectOffsetOnAxis(slots[:, t, k:k + 1], 0),
                                                xn[:, t, :], None).then_inc(xs_scattered[g], 16)

            def gather(q):
                g = q % GROUPS
                for r, n in enumerate(stored_before((q + 1) * CHUNKS)):
                    pool.wait_ge(ys_stored[r], 16 * n)
                for j in range(QUADS):
                    n = q * QUADS + j
                    if n >= 2:
                        pool.wait_ge(y_gathered[n % 2], 16 * 4 * TOPK * (n // 2))
                    for t in range(g * GT + 4 * j, g * GT + 4 * j + 4):
                        for k in range(TOPK):
                            pool.indirect_dma_start(y_tok[:, t, k, :], None, ys_rows[g],
                                                    bass.IndirectOffsetOnAxis(slots[:, t, k:k + 1], 0)
                                                    ).then_inc(y_gathered[n % 2], 16)

            for layer in range(2):
                for g in range(GROUPS):
                    scatter(layer * GROUPS + g)
                for g in range(GROUPS):
                    gather(layer * GROUPS + g)

        @block.scalar
        def _(act):
            def copy(dst, src):
                return act.activation(dst, src, ACT.Copy)

            act.wait_ge(w_transposed, 1)
            copy(attn_wT[:], bank[2][:].rearrange("p (c d) -> p c d", c=4)).then_inc(consts_made, 1)

            def route(q):
                for j in range(QUADS):
                    act.wait_ge(xn_transposed, q * QUADS + j + 1)
                    copy(xnT[:, 512 * j:512 * j + 512], bank[j % 2][:]).then_inc(xnT_ready, 1)
                act.wait_ge(exp_asked, q + 1)
                act.activation(probs[:, :, 0:E], logits[:, :, 0:E], ACT.Exp).then_inc(exp_done, 1)
                for j in range(QUADS):
                    act.wait_ge(shared_h_done, q * QUADS + j + 1)
                    act.activation(sharedT[:, 512 * j:512 * j + 512], bank[2 + j % 2][:], ACT.Gelu,
                                   bias=bs1_col[:]).then_inc(sharedT_ready, 1)
                act.wait_ge(gates_transposed, q + 1)
                copy(gatesT[:].rearrange("p j t -> p (j t)"), bank[0][:]).then_inc(gatesT_ready, 1)

            def run_experts(q):
                g = q % GROUPS

                def store(C, i):
                    wait_chunks(act, ys_ready, C + 1, i)
                    act.dma_start(of_chunk(ys_chunks[g], C - q * CHUNKS, i), ys_out[:, C % RING, :, :]
                                  ).then_inc(ys_stored[C % RING], 16)

                def results(C, i):
                    wait_chunks(act, y_done, C + 1, i)
                    if C >= RING:
                        act.wait_ge(ys_stored[C % RING], 16 * (C // RING) + (i * 16 if not isinstance(i, int) else 0))
                    elif not isinstance(i, int):
                        act.wait_ge(ys_stored[C % RING], i * 16)
                    copy(ys_out[:, C % RING, :, :].rearrange("p u d -> p (u d)"),
                                    bank[4 + C % 2][:, 0:CH * P]).then_inc(ys_ready, 1)

                def step(C, i, head, tail):
                    wait_chunks(act, h_done, C + 1, i)
                    wait_chunks(act, y_done, C - 1, i)
                    for u in range(CH):
                        ins = act.activation(hT[:, C % 2, u * P:(u + 1) * P], bank[2 + C % 2][:, u * P:(u + 1) * P],
                                             ACT.Gelu, bias=w_ring[:, C % RING, u, 2 * F:2 * F + 1])
                    ins.then_inc(hT_ready, 1)
                    if not head:
                        results(C - 1, i)
                    if C - q * CHUNKS >= 2:
                        store(C - 2, i)
                    if tail:
                        store(C - 1, i)
                        results(C, i)
                        store(C, i)

                chunk_steps(act, q, step)

            def attend(g):
                first = g * GT

                def normed(j):
                    n = g * QUADS + j
                    act.wait_ge(norm_ready, n + 1)
                    if n >= 1:
                        act.wait_ge(xa_transposed, n)
                    for i in range(4):
                        ins = act.activation(xa[:, i, :], x[:, first + 4 * j + i, :], ACT.Identity,
                                             bias=shift4[:, i:i + 1], scale=rstd4[:, i:i + 1])
                    ins.then_inc(xa_ready, 1)

                def turned(j):
                    n = g * QUADS + j
                    act.wait_ge(xa_transposed, n + 1)
                    copy(xaT[:, n % 2, :], bank[0][:]).then_inc(xaT_ready, 1)

                def features(t):
                    n = first + t
                    act.wait_ge(qkv_done, n + 1)
                    if n >= 2:
                        act.wait_ge(sums_read, n - 1)
                        act.wait_ge(state_done, n - 1)
                    act.activation(qk_relu[:], bank[1][:, 0:2 * D], ACT.Relu).then_inc(relu_done, 1)
                    copy(v_aug[:, n % 2, :, 0:HD],
                         bank[1][:, 2 * D:3 * D].rearrange("p (h e) -> p h e", h=HEADS))
                    act.wait_ge(relu_done, n + 1)
                    act.activation(qk[:, n % 2, :], qk_relu[:], ACT.Copy, bias=FEATURE_EPS
                                   ).then_inc(features_ready, 1)

                def transposed(t):
                    n = g * (GT + 1) + t
                    act.wait_ge(q_o_transposed, n + 1)
                    lo, hi = (0, 1) if t == 0 else (1, 2) if t == GT else (0, 2)
                    copy(q_oT[:, lo:hi, :], bank[7][:, lo * P:hi * P].rearrange("p (c t) -> p c t", t=P)
                         ).then_inc(q_oT_ready, 1)

                def attended(t):
                    act.wait_ge(projected, first + t + 1)
                    copy(x[:, first + t, :], bank[7][:, 2 * P:3 * P]).then_inc(x_attended, 1)

                normed(0)
                turned(0)
                features(0)
                transposed(0)
                features(1)
                for t in range(GT):
                    if t % 4 == 1 and t + 3 < GT:
                        turned(t // 4 + 1)
                    if t + 2 < GT:
                        features(t + 2)
                    transposed(t + 1)
                    if t % 4 == 0 and t + 4 < GT:
                        normed(t // 4 + 1)
                    attended(t)

            for layer in range(2):
                if layer == 0:
                    route(0)
                    route(1)
                run_experts(2 * layer)
                run_experts(2 * layer + 1)
                if layer == 0:
                    for g in range(GROUPS):
                        attend(g)
                        route(GROUPS + g)

        @block.tensor
        def _(pe):
            pe.wait_ge(consts_made, 1)
            pe.wait_ge(attn_w_loaded, 16 * N_ATTN_W)
            pe.wait_ge(router_w_loaded, 16 * N_ROUTER_W)
            pe.transpose(bank[3][:, 0:E], be1_rows[:], ident[0:E, 0:E])
            for c in range(4):
                ins = pe.transpose(bank[2][:, c * P:(c + 1) * P], attn_rows[:, c, :], ident[:])
            ins.then_inc(w_transposed, 1)

            def route(q):
                g = q % GROUPS
                for j in range(QUADS):
                    pe.wait_ge(xn_ready, q * QUADS + j + 1)
                    if q * QUADS + j >= 2:
                        pe.wait_ge(xnT_ready, q * QUADS + j - 1)
                    for i in range(4):
                        ins = pe.transpose(bank[j % 2][:, i * P:(i + 1) * P], xn[:, g * GT + 4 * j + i, :], ident[:])
                    ins.then_inc(xn_transposed, 1)
                for t in range(GT):
                    if t % 4 == 0:
                        pe.wait_ge(xnT_ready, q * QUADS + t // 4 + 1)
                    ins = pe.matmul(bank[6][:, t * RP:t * RP + E], xnT[:, t * P:(t + 1) * P], wr_sb[:],
                                    start=True, stop=True)
                ins.then_inc(logits_done, 1)
                if q == 0:
                    pe.wait_ge(consts_made, 3)
                for j in range(QUADS):
                    if q * QUADS + j >= 2:
                        pe.wait_ge(sharedT_ready, q * QUADS + j - 1)
                    pe.matmul(bank[2 + j % 2][:], ws1_sb[:], xnT[:, 512 * j:512 * j + 512],
                              start=True, stop=True).then_inc(shared_h_done, 1)
                pe.wait_ge(chosen_ready, q + 1)
                pe.matmul(bank[7][:, 0:GT * E], before[:], chosen[:].rearrange("p t e -> p (t e)"),
                          start=True, stop=False, skip_group_check=True)
                for s in range(1, GT):
                    pe.matmul(bank[7][:, s * E:GT * E], ones[:], chosen[:, 0:GT - s, :].rearrange("p t e -> p (t e)"),
                              start=False, stop=s == GT - 1, skip_group_check=True)
                for t in range(GT):
                    ins = pe.matmul(bank[6][:, 0:E], ones[:], chosen[:, t, :], start=t == 0, stop=t == GT - 1)
                ins.then_inc(ranks_done, 1)
                pe.wait_ge(gates_ready, q + 1)
                for j in range(QUADS):
                    ins = pe.transpose(bank[0][:, j * P:(j + 1) * P],
                                       gates[:, 4 * j:4 * j + 4, :].rearrange("p t e -> p (t e)"), ident[:])
                ins.then_inc(gates_transposed, 1)
                pe.wait_ge(tile_expert_ready, q + 1)
                pe.matmul(bank[6][0:1, P:2 * P], tile_expert[:], ident[:], start=True, stop=True
                          ).then_inc(expert_row_done, 1)
                pe.wait_ge(gatesT_ready, q + 1)
                for j in range(QUADS):
                    pe.wait_ge(sharedT_ready, q * QUADS + j + 1)
                    if q * QUADS + j >= 2:
                        pe.wait_ge(shared_out_read, q * QUADS + j - 1)
                    for i in range(4):
                        o = bank[4 + j % 2][:, i * P:(i + 1) * P]
                        t = 4 * j + i
                        pe.matmul(o, sharedT[:, t * P:(t + 1) * P], ws2_sb[:], start=True, stop=False)
                        ins = pe.matmul(o, gatesT[:, j, :], be2_aug[:, i, :],
                                        start=False, stop=True)
                    ins.then_inc(shared_out_done, 1)

            def run_experts(q):
                pe.wait_ge(router_done, 2 * (q // 2 + 1))

                def transposes(C, i):
                    r = C % RING
                    pe.wait_ge(xs_loaded[r], 16 * (C // RING + 1) + (i * 16 if not isinstance(i, int) else 0))
                    wait_chunks(pe, xsT_ready, C - 1, i)
                    for u in range(CH):
                        ins = pe.transpose(bank[C % 2][:, u * P:(u + 1) * P], xs_in[:, r, u, :], ident[:])
                    ins.then_inc(xs_transposed, 1)

                def down(C, i):
                    wait_chunks(pe, hT_ready, C + 1, i)
                    wait_chunks(pe, ys_ready, C - 1, i)
                    for u in range(CH):
                        ins = pe.matmul(bank[4 + C % 2][:, u * P:(u + 1) * P], hT[:, C % 2, u * P:(u + 1) * P],
                                        w_ring[:, C % RING, u, F:2 * F], start=True, stop=True)
                    ins.then_inc(y_done, 1)

                def step(C, i, head, tail):
                    if head:
                        transposes(C, i)
                    if not tail:
                        transposes(C + 1, i)
                    wait_chunks(pe, xsT_ready, C + 1, i)
                    wait_chunks(pe, weights_copied, C + 1, i)
                    wait_chunks(pe, hT_ready, C - 1, i)
                    for u in range(CH):
                        ins = pe.matmul(bank[2 + C % 2][:, u * P:(u + 1) * P], w_ring[:, C % RING, u, 0:F],
                                        xsT[:, C % 2, u * P:(u + 1) * P], start=True, stop=True)
                    ins.then_inc(h_done, 1)
                    if not head:
                        down(C - 1, i)
                    if tail:
                        down(C, i)

                chunk_steps(pe, q, step)

            def attend(g):
                first = g * GT
                burst0 = g * (GT + 1)

                def quad(j):
                    n = g * QUADS + j
                    pe.wait_ge(xa_ready, n + 1)
                    if n >= 1:
                        pe.wait_ge(xaT_ready, n)
                    for i in range(4):
                        ins = pe.transpose(bank[0][:, i * P:(i + 1) * P], xa[:, i, :], ident[:])
                    ins.then_inc(xa_transposed, 1)

                def project(t):
                    n = first + t
                    if t % 4 == 0:
                        pe.wait_ge(xaT_ready, n // 4 + 1)
                    if n >= 1:
                        pe.wait_ge(features_ready, n)
                    o = bank[1][:, 0:3 * D]
                    pe.matmul(o, xaT[:, (n // 4) % 2, (t % 4) * P:(t % 4 + 1) * P],
                              attn_wT[:, 0:3, :].rearrange("p c d -> p (c d)"), start=True, stop=False)
                    pe.matmul(o, ones_row[:], qkv_bias[:], start=False, stop=True).then_inc(qkv_done, 1)

                def running_sums(t):
                    n = first + t
                    pe.wait_ge(kv_ready, n + 1)
                    if n >= 1:
                        pe.wait_ge(sums_read, n)
                    for c, (a, b) in enumerate(HEAD_CUTS):
                        ins = pe.matmul(bank[2 + c][:, 0:(b - a) * HA * HD], tri[:],
                                        kv[:, n % 2, a:b, :, :].rearrange("p h e d -> p (h e d)"),
                                        start=True, stop=True)
                    ins.then_inc(sums_done, 1)
                    if n >= 1:
                        pe.wait_ge(state_ready, n - n // BT)
                    pe.matmul(bank[5][:, 0:HEADS * HA], qk[:, n % 2, D:2 * D],
                              v_aug[:, n % 2, :, :].rearrange("p h e -> p (h e)"), start=t % BT == 0,
                              stop=True, skip_group_check=True).then_inc(state_done, 1)

                def burst(t):
                    n = burst0 + t
                    if t > 0:
                        pe.wait_ge(attn_o_ready, first + t)
                    if n >= 1:
                        pe.wait_ge(x_attended, first + max(t - 1, 0))
                        pe.wait_ge(q_oT_ready, n)
                    if t < GT:
                        pe.wait_ge(features_ready, first + t + 1)
                        ins = pe.transpose(bank[7][:, 0:P], qk[:, (first + t) % 2, 0:D], ident[:])
                    if t > 0:
                        ins = pe.transpose(bank[7][:, P:2 * P], attn_o[:], ident[:])
                    ins.then_inc(q_o_transposed, 1)
                    pe.wait_ge(q_oT_ready, n + 1)
                    if t % BT and t < GT:
                        done = (first + t) - (first + t) // BT
                        pe.wait_ge(state_ready, done)
                        if done > 1:
                            pe.wait_ge(carried_read, done - 1)
                        pe.matmul(bank[6][:, 0:HEADS * HA], q_oT[:, 0, :], state[:], start=True, stop=True
                                  ).then_inc(carried_done, 1)
                    if t > 0:
                        o = bank[7][:, 2 * P:3 * P]
                        pe.matmul(o, q_oT[:, 1, :], attn_wT[:, 3, :], start=True, stop=False)
                        pe.matmul(o, ones_row[:], out_bias[:], start=False, stop=False)
                        pe.matmul(o, ident[:], x[:, first + t - 1, :], start=False, stop=True).then_inc(projected, 1)

                quad(0)
                project(0)
                burst(0)
                project(1)
                running_sums(0)
                project(2)
                for t in range(GT):
                    if t % 4 == 1 and t + 3 < GT:
                        quad(t // 4 + 1)
                    if t + 1 < GT:
                        running_sums(t + 1)
                    burst(t + 1)
                    if t + 3 < GT:
                        project(t + 3)

            for layer in range(2):
                if layer == 0:
                    route(0)
                    route(1)
                run_experts(2 * layer)
                run_experts(2 * layer + 1)
                if layer == 0:
                    for g in range(GROUPS):
                        attend(g)
                        route(GROUPS + g)

        @block.vector
        def _(dve):
            steps = [0]

            def link(ins):
                steps[0] += 1
                ins.then_inc(dve_step, 1)
                dve.wait_ge(dve_step, steps[0])

            NORM_STAGES = 17

            def norm_stage(k, first, n, at=0):
                m, v, r, a, b = (s[:, 0:n] for s in (mean, var, rstd, tmp_a, tmp_b))
                s, y0 = stats[:, 0:n, :], seed[:, 0:n].bitcast(F32)
                if k == 0:
                    for t in range(n):
                        ins = dve.bn_stats(stats[:, t, :], x[:, first + t, :])
                elif k == 1:
                    dve.tensor_tensor(a, s[:, :, 1], s[:, :, 4], ALU.subtract)
                    dve.tensor_tensor(b, s[:, :, 2], s[:, :, 5], ALU.add)
                    ins = dve.tensor_tensor(r, s[:, :, 1], s[:, :, 4], ALU.add)
                elif k == 2:
                    dve.tensor_scalar(m, r, 0.5, None, ALU.mult)
                    dve.tensor_scalar(v, b, 1.0 / D, LN_EPS, ALU.mult, ALU.add)
                    ins = dve.scalar_tensor_tensor(out=seed_f[:, 0:n], in0=a, scalar=0.25, in1=a,
                                                   op0=ALU.mult, op1=ALU.mult)
                elif k == 3:
                    ins = dve.tensor_tensor(v, v, seed_f[:, 0:n], ALU.add)
                elif k == 4:
                    ins = dve.tensor_scalar(seed[:, 0:n], v.bitcast(I32), 1, None, ALU.logical_shift_right)
                elif k == 5:
                    ins = dve.tensor_copy(seed_f[:, 0:n], seed[:, 0:n])
                elif k == 6:
                    ins = dve.tensor_scalar(seed[:, 0:n], seed_f[:, 0:n], -1.0, float(RSQRT_SEED), ALU.mult, ALU.add)
                elif k < 16:
                    y = y0 if k < 10 else r
                    if (k - 7) % 3 == 0:
                        ins = dve.tensor_tensor(a, y, y, ALU.mult)
                    elif (k - 7) % 3 == 1:
                        ins = dve.scalar_tensor_tensor(out=b, in0=a, scalar=-0.5, in1=v, op0=ALU.mult, op1=ALU.mult)
                    else:
                        ins = dve.scalar_tensor_tensor(out=r, in0=b, scalar=1.5, in1=y, op0=ALU.add, op1=ALU.mult)
                else:
                    ins = dve.scalar_tensor_tensor(out=shift[:, at:at + n], in0=m, scalar=-1.0, in1=r,
                                                   op0=ALU.mult, op1=ALU.mult)
                return ins

            def norm_stats(first, n):
                for k in range(NORM_STAGES - 1):
                    link(norm_stage(k, first, n))

            def over_tiles(a):
                return a.unsqueeze(1).broadcast_to([P, GT, E])

            def route(q):
                g = q % GROUPS
                first = g * GT
                if q < GROUPS:
                    dve.wait_ge(x_loaded[g], 16)
                else:
                    dve.wait_ge(x_attended, first + GT)
                norm_stats(first, GT)
                if q >= GROUPS:
                    dve.wait_ge(xs_scattered[g], 16 * GT * TOPK * (q // GROUPS))
                for t in range(GT):
                    ins = dve.tensor_scalar(xn[:, first + t, :], x[:, first + t, :], mean[:, t:t + 1],
                                            rstd[:, t:t + 1], ALU.subtract, ALU.mult)
                    if t % 4 == 3:
                        ins.then_inc(xn_ready, 1)
                dve.wait_ge(xn_ready, QUADS * (q + 1))
                xg = x[:, first:first + GT, :]
                link(dve.scalar_tensor_tensor(out=xg, in0=xn[:, first:first + GT, :], scalar=0.5, in1=xg,
                                              op0=ALU.mult, op1=ALU.add))
                if q == 0:
                    dve.wait_ge(w_transposed, 1)
                    dve.tensor_copy(experts[:, :, 2 * F], bank[3][:, 0:E]).then_inc(consts_made, 1)
                    dve.wait_ge(router_w_loaded, 16 * N_ROUTER_W)
                lg, pr = logits[:, :, 0:E], probs[:, :, 0:E]
                dve.wait_ge(logits_done, q + 1)
                link(dve.tensor_tensor(lg, bank[6][:].rearrange("p (t e) -> p t e", e=RP)[:, :, 0:E],
                                       over_tiles(br_all[:]), ALU.add))
                link(dve.tensor_reduce(row_max[:], lg, AXX, ALU.max))
                dve.tensor_tensor(lg, lg, row_max[:].unsqueeze(2).broadcast_to([P, GT, E]), ALU.subtract
                                  ).then_inc(exp_asked, 1)
                dve.wait_ge(exp_done, q + 1)
                link(dve.tensor_reduce(row_sum[:], pr, AXX, ALU.add))
                link(dve.reciprocal(row_sum[:], row_sum[:]))
                link(dve.tensor_tensor(pr, pr, row_sum[:].unsqueeze(2).broadcast_to([P, GT, E]), ALU.mult))
                for t in range(GT):
                    ins = dve.max(top[:, t, :], probs[:, t, 0:E])
                link(ins)
                for t in range(GT):
                    ins = dve.max_index(top_id[:, t, :], top[:, t, :], probs[:, t, 0:E])
                link(dve.tensor_scalar(half_gate[:, first:first + GT, :], top[:, :, 0:TOPK], 0.5, None, ALU.mult))
                link(dve.tensor_copy(top_idf[:], top_id[:, :, 0:TOPK]))
                link(dve.tensor_tensor(one_hot[:], top_idf[:].unsqueeze(3).broadcast_to([P, GT, TOPK, E]),
                                       expert_ids[:].unsqueeze(1).unsqueeze(1).broadcast_to([P, GT, TOPK, E]),
                                       ALU.is_equal))
                link(dve.tensor_tensor(chosen_a[:], one_hot[:, :, 0, :], one_hot[:, :, 1, :], ALU.add))
                dve.tensor_tensor(chosen[:], chosen_a[:], one_hot[:, :, 2, :], ALU.add).then_inc(chosen_ready, 1)
                dve.wait_ge(chosen_ready, q + 1)
                dve.tensor_tensor(gates[:, :, 0:E], pr, chosen[:], ALU.mult).then_inc(gates_ready, 1)
                dve.wait_ge(ranks_done, q + 1)
                link(dve.tensor_scalar(count_i[:], bank[6][:, 0:E], float(P - 1), None, ALU.add))
                link(dve.tensor_scalar(count_t[:], count_i[:], 7, None, ALU.logical_shift_right))
                link(dve.tensor_copy(run_tiles[:], count_t[:]))
                link(dve.tensor_tensor_scan(run_end[:], run_tiles[:], zero_row[:], 0.0, ALU.add, ALU.add))
                dve.tensor_scalar(ended[:], run_end[:], row_id[:, 0:1], None, ALU.is_le)
                link(dve.tensor_tensor(run_base[:], run_end[:], run_tiles[:], ALU.subtract))
                link(dve.tensor_reduce(tile_expert[:], ended[:], AXX, ALU.add))
                dve.tensor_scalar(tile_expert[:], tile_expert[:], float(E - 1), None, ALU.min
                                  ).then_inc(tile_expert_ready, 1)
                link(dve.tensor_scalar(run_base[:], run_base[:], float(P), None, ALU.mult))
                link(dve.tensor_tensor(slot_of[:], bank[7][:, 0:GT * E].rearrange("p (t e) -> p t e", e=E),
                                       over_tiles(run_base[:]), ALU.add))
                link(dve.tensor_tensor(hot_slots[:], one_hot[:],
                                       slot_of[:].unsqueeze(2).broadcast_to([P, GT, TOPK, E]), ALU.mult))
                link(dve.tensor_reduce(slot_f[:], hot_slots[:], AXX, ALU.add))
                dve.tensor_copy(slots[:, first:first + GT, :], slot_f[:]).then_inc(slots_ready, 1)
                dve.wait_ge(expert_row_done, q + 1)
                link(dve.tensor_copy(expert_tab[0:1, g * P:g * P + P], bank[6][0:1, P:2 * P]))
                for j in range(QUADS):
                    dve.wait_ge(shared_out_done, q * QUADS + j + 1)
                    xq = x[:, first + 4 * j:first + 4 * j + 4, :].rearrange("p t d -> p (t d)")
                    dve.scalar_tensor_tensor(out=xq, in0=bank[4 + j % 2][:], scalar=0.5, in1=xq,
                                             op0=ALU.mult, op1=ALU.add).then_inc(shared_out_read, 1)
                dve.wait_ge(shared_out_read, QUADS * (q + 1))
                dve.tensor_copy(tmp_b[:], row_max[:]).then_inc(router_done, 1)
                dve.wait_ge(router_done, q + 1)

            def run_experts(q):
                g = q % GROUPS

                def expert_ids_of(c, n, i):
                    at = g * P + c * CH
                    at = slice(at, at + n * CH) if isinstance(i, int) else bass.ds(i * (RING * CH) + at, n * CH)
                    _, ids = nc.values_load_multi_w_load_instructions(
                        expert_tab[0:1, at], engines=(mybir.EngineType.DVE,), min_val=0, max_val=E - 1,
                        skip_runtime_bounds_check_because="the table's values are capped at E - 1")
                    return {c + k: ids[k * CH:(k + 1) * CH] for k in range(n)}

                def weights(C, i):
                    wait_chunks(dve, y_done, C - RING + 1, i)
                    for u, e in enumerate(ids[C - q * CHUNKS]):
                        ins = dve.tensor_copy(w_ring[:, C % RING, u:u + 1, :], experts[:, bass.ds(e, 1), :])
                    ins.then_inc(weights_copied, 1)

                def turned(C, i):
                    wait_chunks(dve, xs_transposed, C + 1, i)
                    wait_chunks(dve, h_done, C - 1, i)
                    dve.tensor_copy(xsT[:, C % 2, :], bank[C % 2][:, 0:CH * P]).then_inc(xsT_ready, 1)

                ids = {}

                def step(C, i, head, tail):
                    c = C - q * CHUNKS
                    if c < 2 or (c - 2) % RING == 0:
                        a, b = (0, 2) if c == 0 else (2, 3) if c == 1 else (c + 1, min(c + 1 + RING, CHUNKS))
                        ids.update(expert_ids_of(a, b - a, i))
                    if head:
                        weights(C, i)
                        turned(C, i)
                    if not tail:
                        weights(C + 1, i)
                        turned(C + 1, i)

                if q == 0:
                    dve.wait_ge(experts_loaded, 32)
                chunk_steps(dve, q, step)

            def add_choice(q, j, k):
                n = q * QUADS + j
                if k == 0:
                    dve.wait_ge(y_gathered[n % 2], 16 * 4 * TOPK * (n // 2 + 1))
                first = (q % GROUPS) * GT + 4 * j
                for t in range(first, first + 4):
                    ins = dve.scalar_tensor_tensor(out=x[:, t, :], in0=y_tok[:, t, k, :],
                                                   scalar=half_gate[:, t, k:k + 1], in1=x[:, t, :],
                                                   op0=ALU.mult, op1=ALU.add)
                return ins

            QUAD_STAGES = TOPK + NORM_STAGES

            def attend(g):
                first = g * GT
                quad_step = [0]

                def mark(ins):
                    steps[0] += 1
                    ins.then_inc(dve_step, 1)
                    return steps[0]

                def quad_stage(j, k):
                    n = g * QUADS + j
                    if k > 0:
                        dve.wait_ge(dve_step, quad_step[0])
                    if k < TOPK:
                        ins = add_choice(g, j, k)
                    else:
                        ins = norm_stage(k - TOPK, first + 4 * j, 4)
                    quad_step[0] = mark(ins)
                    if k == QUAD_STAGES - 1:
                        dve.wait_ge(dve_step, quad_step[0])
                        if n >= 1:
                            dve.wait_ge(xa_ready, n)
                        dve.tensor_copy(rstd4[:], rstd[:, 0:4])
                        dve.tensor_copy(shift4[:], shift[:, 0:4]).then_inc(norm_ready, 1)

                def gap(t, k):
                    if t == 0:
                        for i in range(4 * k, 4 * k + 4):
                            quad_stage(1, i)
                    elif t <= GT - 8 + 4:
                        j = (t + 3) // 4 + 1
                        if j < QUADS:
                            quad_stage(j, 5 * ((t + 3) % 4) + k)

                def outer(t):
                    n = first + t
                    dve.wait_ge(features_ready, n + 1)
                    if n >= 2:
                        dve.wait_ge(sums_done, n - 1)
                    k = qk[:, n % 2, D:2 * D].rearrange("p (h d) -> p h d", h=HEADS)
                    dve.tensor_tensor(kv[:, n % 2, :, :, :], k.unsqueeze(2).broadcast_to([P, HEADS, HA, HD]),
                                      v_aug[:, n % 2, :, :].unsqueeze(3).broadcast_to([P, HEADS, HA, HD]), ALU.mult
                                      ).then_inc(kv_ready, 1)

                def apply(t):
                    n = first + t
                    dve.wait_ge(sums_done, n + 1)
                    qh = qk[:, n % 2, 0:D].rearrange("p (h d) -> p h d", h=HEADS)
                    for c, (a, b) in enumerate(HEAD_CUTS):
                        s = bank[2 + c][:, 0:(b - a) * HA * HD].rearrange("p (h e d) -> p h e d", e=HA, d=HD)
                        ins = dve.tensor_tensor(weighed[:, a:b, :, :], s,
                                                qh[:, a:b, :].unsqueeze(2).broadcast_to([P, b - a, HA, HD]), ALU.mult)
                    ins.then_inc(sums_read, 1)
                    gap(t, 1)
                    dve.wait_ge(sums_read, n + 1)
                    summed = mark(dve.tensor_reduce(num_den[:], weighed[:], AXX, ALU.add))
                    gap(t, 2)
                    dve.wait_ge(dve_step, summed)
                    if t % BT:
                        dve.wait_ge(carried_done, n - n // BT)
                        nd = num_den[:].rearrange("p h e -> p (h e)")
                        ins = dve.tensor_tensor(nd, nd, bank[6][:, 0:HEADS * HA], ALU.add)
                        ins.then_inc(carried_read, 1)
                        gap(t, 3)
                        dve.wait_ge(carried_read, n - n // BT)
                    else:
                        gap(t, 3)
                    guarded = mark(dve.tensor_scalar(den[:], num_den[:, :, HD], DEN_EPS, None, ALU.max))
                    gap(t, 4)
                    dve.wait_ge(dve_step, guarded)
                    inverted = mark(dve.reciprocal(den_inv[:], den[:]))
                    if t % BT != BT - 1:
                        dve.wait_ge(state_done, n + 1)
                        dve.tensor_tensor(state[:], bank[5][:, 0:HEADS * HA],
                                          head_mask[:].rearrange("p h e -> p (h e)"), ALU.mult
                                          ).then_inc(state_ready, 1)
                    dve.wait_ge(dve_step, inverted)
                    if n >= 1:
                        dve.wait_ge(q_o_transposed, g * (GT + 1) + t + min(t, 1))
                    dve.tensor_tensor(attn_o[:].rearrange("p (h e) -> p h e", h=HEADS), num_den[:, :, 0:HD],
                                      den_inv[:].unsqueeze(2).broadcast_to([P, HEADS, HD]), ALU.mult
                                      ).then_inc(attn_o_ready, 1)

                for k in range(QUAD_STAGES):
                    quad_stage(0, k)
                outer(0)
                for t in range(GT):
                    if t + 1 < GT:
                        outer(t + 1)
                    gap(t, 0)
                    apply(t)

            for layer in range(2):
                if layer == 0:
                    route(0)
                    route(1)
                run_experts(2 * layer)
                run_experts(2 * layer + 1)
                for g in range(GROUPS):
                    if layer == 0:
                        attend(g)
                        route(GROUPS + g)
                    else:
                        for j in range(QUADS):
                            for k in range(TOPK - 1):
                                link(add_choice(GROUPS + g, j, k))
                            add_choice(GROUPS + g, j, TOPK - 1).then_inc(x_final, 1)


_INS = ['L0_attn_x', 'L0_attn_qkv_w', 'L0_attn_qkv_b', 'L0_attn_out_w', 'L0_attn_out_b',
        'L0_ffn_ws1', 'L0_ffn_bs1', 'L0_ffn_ws2', 'L0_ffn_bs2', 'L0_ffn_We1', 'L0_ffn_Be1',
        'L0_ffn_We2', 'L0_ffn_Be2', 'L0_ffn_Wr', 'L0_ffn_br']


def kernel(**inputs):
    import numpy as _np
    import concourse.bacc as _bacc
    from concourse import mybir as _mybir
    from concourse.bass_utils import run_bass_kernel_spmd as _run

    nc = _bacc.Bacc("TRN2", target_bir_lowering=False, num_devices=1)
    arrays, args = {}, []
    for name in _INS:
        a = _np.ascontiguousarray(inputs[name])
        arrays[f"in_{name}_dram"] = a
        args.append(nc.dram_tensor(f"in_{name}_dram", a.shape, _mybir.dt.from_np(a.dtype), kind="ExternalInput").ap())
    shape = inputs['L0_attn_x'].shape
    args.append(nc.dram_tensor("out_0_dram", shape, _mybir.dt.float32, kind="ExternalOutput").ap())
    macaron_kernel(nc, *args)
    r = _run(nc, [arrays], core_ids=[0])
    return r.results[0]["out_0_dram"]
```

```python
from contextlib import ExitStack

import concourse.bass as bass
from concourse import mybir

F32 = mybir.dt.float32
BF16 = mybir.dt.bfloat16
I32 = mybir.dt.int32
U32 = mybir.dt.uint32
ALU = mybir.AluOpType
ACT = mybir.ActivationFunctionType
AXX = mybir.AxisListType.X

P = 128
LN_EPS = 1e-5
FEATURE_EPS = 1e-6
DEN_EPS = 1e-6
RSQRT_SEED = 0x5F3759DF


def macaron_kernel(nc, x_in, qkv_w, qkv_b, out_w, out_b, ws1, bs1, ws2, bs2,
                   we1, be1, we2, be2, wr, br, out):
    BATCH, SEQ, D = x_in.shape
    E, _, F = we1.shape
    TOPK = 3
    HEADS, HD = 16, D // 16
    HA = HD + 1
    TILES = BATCH * SEQ // P
    GROUPS = 2
    GT = TILES // GROUPS
    BT = SEQ // P
    QUADS = GT // 4
    EARLY_QUADS = 2
    EARLY = 4 * EARLY_QUADS
    SLOT_PARTS = [(0, 4), (4, GT)]
    PAIRS = GT * P * TOPK
    SLOT_TILES = PAIRS // P - 1 + E
    CH = 3
    CHUNKS = SLOT_TILES // CH
    RING = 4
    RP = 32
    W_COLS = 2 * F + 1
    assert D == P and F == P and SLOT_TILES % CH == 0 and (CHUNKS - 2) % RING == 0
    HEAD_CUTS = [(0, 6), (6, 11), (11, 16)]
    CUTS = len(HEAD_CUTS)

    x_tok = x_in.rearrange("b (t p) d -> p (b t) d", p=P)
    out_tok = out.rearrange("b (t p) d -> p (b t) d", p=P)
    def scratch(name):
        rows = [nc.dram_tensor(f"{name}{g}", [SLOT_TILES * P, D], F32, kind="Internal").ap() for g in range(GROUPS)]
        return rows, [r.rearrange("(c u p) d -> p c u d", u=CH, p=P) for r in rows]

    xs_rows, xs_chunks = scratch("xs_rows")
    ys_rows, ys_chunks = scratch("ys_rows")

    with ExitStack() as ctx:
        def sb(name, shape, dt=F32):
            return ctx.enter_context(nc.sbuf_tensor(name, shape, dt))

        def sem(name):
            return ctx.enter_context(nc.semaphore(name))

        bank = [ctx.enter_context(nc.psum_tensor(f"bank{i}", [P, 512], F32)) for i in range(8)]

        experts = sb("experts", [P, E, W_COLS])
        be1_rows = sb("be1_rows", [E, F])
        be2_aug = sb("be2_aug", [P, 4, D])
        wr_sb = sb("wr_sb", [P, E])
        br_all = sb("br_all", [P, E])
        ws1_sb = sb("ws1_sb", [P, F])
        ws2_sb = sb("ws2_sb", [P, D])
        bs1_col = sb("bs1_col", [P, 1])
        attn_wT = sb("attn_wT", [P, 4, D])
        bias_row = sb("bias_row", [1, 4 * D])
        bias_parts = sb("bias_parts", [1, 3, 4 * D], BF16)
        bias3 = sb("bias3", [3, 4 * D], BF16)
        ident = sb("ident", [P, P])
        tri = sb("tri", [P, P])
        before = sb("before", [P, P], BF16)
        ones = sb("ones", [P, P], BF16)
        head_mask = sb("head_mask", [P, HEADS, HA])
        expert_ids = sb("expert_ids", [P, E], BF16)
        row_id = sb("row_id", [P, 1])

        x = sb("x", [P, TILES, D])
        xn = sb("xn", [P, TILES, D])
        xnT = sb("xnT", [P, GT * P])
        sharedT = sb("sharedT", [P, GT * P])

        def norm_buffers(name, n):
            return [sb(f"{name}_stats", [P, n, 6])] + [
                sb(f"{name}_{what}", [P, n], I32 if what == "bits" else F32)
                for what in ("mean", "var", "rstd", "a", "b", "bits", "bits_value", "shift")]

        group_norm = norm_buffers("group", GT)
        quad_norm = norm_buffers("quad", 4)
        exp_table = sb("exp_table", [P, 1])
        rstd4 = sb("rstd4", [P, 4])
        shift4 = sb("shift4", [P, 4])
        logits = sb("logits", [P, GT, RP])
        probs = sb("probs", [P, GT, RP])
        row_max = sb("row_max", [P, GT])
        row_sum = sb("row_sum", [P, GT])
        top = sb("top", [P, GT, 8])
        top_id = sb("top_id", [P, GT, 8], U32)
        top_idf = sb("top_idf", [P, GT, TOPK], BF16)
        one_hot = sb("one_hot", [P, GT, TOPK, E], BF16)
        hot_slots = sb("hot_slots", [P, GT, TOPK, E])
        chosen_a = sb("chosen_a", [P, GT, E], BF16)
        chosen = sb("chosen", [P, GT, E], BF16)
        gates = sb("gates", [P, GROUPS, GT, RP])
        gatesT = sb("gatesT", [P, QUADS, P])
        half_gate = sb("half_gate", [P, TILES, TOPK])
        count_i = sb("count_i", [P, E], I32)
        count_t = sb("count_t", [P, E], I32)
        run_tiles = sb("run_tiles", [P, E])
        run_end = sb("run_end", [P, E])
        run_base = sb("run_base", [P, E])
        zero_row = sb("zero_row", [P, E])
        slot_of = sb("slot_of", [P, GT, E])
        slot_f = sb("slot_f", [P, GT, TOPK])
        slots = sb("slots", [P, TILES, TOPK], U32)
        ended = sb("ended", [P, E])
        tile_expert = sb("tile_expert", [P, 1])
        expert_tab = sb("expert_tab", [1, GROUPS * P], I32)
        y_tok = sb("y_tok", [P, TILES, TOPK, D])

        y_flat = y_tok[:].rearrange("p t k d -> p (t k d)")
        attn_rows = y_flat[:, 0:4 * D].rearrange("p (c d) -> p c d", d=D)

        xs_in = sb("xs_in", [P, RING, CH, D])
        xsT = sb("xsT", [P, 2, CH * P])
        w_ring = sb("w_ring", [P, RING, CH, W_COLS])
        hT = sb("hT", [P, 2, CH * P])
        ys_out = sb("ys_out", [P, RING, CH, D])

        zeros = ys_out[:, 0, 0, :]

        xa = xnT[:, EARLY * P:EARLY * P + 4 * D].rearrange("p (t d) -> p t d", d=D)
        xaT = ys_out[:].rearrange("p r u d -> p (r u d)")[:, 0:8 * D].rearrange("p (b n) -> p b n", b=2)
        qk_relu = sb("qk_relu", [P, 2 * D])
        qk = sb("qk", [P, 2, 2 * D])
        bias_part = qk[0:1].rearrange("p b n -> p (b n)")
        v_aug = sb("v_aug", [P, 2, HEADS, HA])
        kv = w_ring[:].rearrange("p r u w -> p (r u w)")[:, 0:2 * HEADS * HA * HD].rearrange(
            "p (b h e d) -> p b h e d", b=2, e=HA, d=HD)
        weighed = hot_slots[:].rearrange("p t k e -> p (t k e)")[:, 0:HEADS * HA * HD].rearrange(
            "p (h e d) -> p h e d", e=HA, d=HD)
        num_den = sb("num_den", [P, HEADS, HA])
        den = sb("den", [P, HEADS])
        den_inv = sb("den_inv", [P, HEADS])
        attn_o = sb("attn_o", [P, D])
        q_oT = sb("q_oT", [P, 2, P])
        state = sb("state", [P, HEADS * HA])

        x_loaded = [sem(f"x_loaded{g}") for g in range(GROUPS)]
        x_early_loaded = sem("x_early_loaded")
        wr_loaded = sem("wr_loaded")
        router_w_loaded = sem("router_w_loaded")
        attn_w_loaded = sem("attn_w_loaded")
        experts_loaded = sem("experts_loaded")
        bias_split = sem("bias_split")
        bias_loaded = sem("bias_loaded")
        zeros_made = sem("zeros_made")
        slots_zeroed = [sem(f"slots_zeroed{g}") for g in range(GROUPS)]
        consts_made = sem("consts_made")
        pool_step = sem("pool_step")
        dve_step = sem("dve_step")
        w_transposed = sem("w_transposed")
        xn_ready = sem("xn_ready")
        xn_ready_act = sem("xn_ready_act")
        xn_transposed = sem("xn_transposed")
        xnT_ready = sem("xnT_ready")
        logits_done = sem("logits_done")
        exp_asked = sem("exp_asked")
        exp_done = sem("exp_done")
        chosen_ready = sem("chosen_ready")
        gates_ready = sem("gates_ready")
        counts_done = sem("counts_done")
        ranks_done = sem("ranks_done")
        slots_ready = sem("slots_ready")
        tile_expert_ready = sem("tile_expert_ready")
        expert_row_done = sem("expert_row_done")
        shared_h_done = sem("shared_h_done")
        sharedT_ready = sem("sharedT_ready")
        gates_transposed = sem("gates_transposed")
        gatesT_ready = sem("gatesT_ready")
        shared_out_done = sem("shared_out_done")
        shared_out_read = sem("shared_out_read")
        normed_added = sem("normed_added")
        xs_scattered = [sem(f"xs_scattered{g}") for g in range(GROUPS)]
        xs_loaded = [sem(f"xs_loaded{r}") for r in range(RING)]
        xs_transposed = sem("xs_transposed")
        xsT_ready = sem("xsT_ready")
        weights_copied = sem("weights_copied")
        h_done = sem("h_done")
        hT_ready = sem("hT_ready")
        y_done = sem("y_done")
        ys_ready = sem("ys_ready")
        ys_stored = [sem(f"ys_stored{r}") for r in range(RING)]
        y_gathered = [sem(f"y_gathered{r}") for r in range(2)]
        norm_ready = sem("norm_ready")
        xa_ready = sem("xa_ready")
        group_norm_ready = sem("group_norm_ready")
        xa_transposed = sem("xa_transposed")
        xaT_ready = sem("xaT_ready")
        qkv_done = sem("qkv_done")
        relu_done = sem("relu_done")
        features_ready = sem("features_ready")
        kv_ready = sem("kv_ready")
        sums_done = sem("sums_done")
        sums_read = sem("sums_read")
        state_done = sem("state_done")
        state_ready = sem("state_ready")
        attn_o_ready = sem("attn_o_ready")
        q_o_transposed = sem("q_o_transposed")
        q_oT_ready = sem("q_oT_ready")
        carried_done = sem("carried_done")
        carried_read = sem("carried_read")
        projected = sem("projected")
        x_attended = sem("x_attended")
        y_gathered_last = [sem(f"y_gathered_last{i}") for i in range(4)]
        x_final = sem("x_final")
        out_stored = sem("out_stored")

        N_ROUTER_W = 5 + 8
        N_ATTN_W = 4
        N_EXPERT_W = 3

        def stored_before(c):
            return [(c - r + RING - 1) // RING for r in range(RING)]

        def chunk_steps(eng, q, step):
            first = q * CHUNKS
            for c in range(2):
                step(first + c, 0, c == 0, False)
            loops = (CHUNKS - 2) // RING - (4 if q == 1 else 1)
            with eng.Fori(0, loops) as i:
                for c in range(RING):
                    step(first + 2 + c, i, False, False)
            for c in range(2 + RING * loops, CHUNKS):
                step(first + c, 0, False, c == CHUNKS - 1)

        def of_chunk(chunks, c, i):
            if isinstance(i, int):
                return chunks[:, c + RING * i, :, :]
            return chunks[:, bass.ds(i * RING + c, 1), :, :].rearrange("p c u d -> p (c u) d")

        def wait_chunks(eng, semaphore, n, i, each=1):
            if isinstance(i, int):
                if n + RING * i > 0:
                    eng.wait_ge(semaphore, each * (n + RING * i))
            else:
                eng.wait_ge(semaphore, i * (RING * each) + each * n)

        SHARED_ORDER = [0, 1, 3, 2]
        TURN_AGAIN = 2 * GROUPS

        def shared_before(q):
            return SHARED_ORDER.index(q)

        def normed_by_act(q, j):
            return j % 2 == 1 or (q >= GROUPS and j < EARLY_QUADS)

        def xn_count(q, j):
            return sum(normed_by_act(p, i) == normed_by_act(q, j)
                       for p in range(q + 1) for i in range(QUADS) if p < q or i <= j)

        def norm_count(q, early=False):
            return sum(1 if p == 1 else 2 for p in range(q + 1)) - (1 if early else 0)

        def xnT_bank(q, j):
            return bank[0 if GROUPS <= q < TURN_AGAIN and j <= EARLY_QUADS else j % 2]

        def softmax_parts(q):
            parts = [(0, GT)] if q == 1 else [(0, EARLY), (EARLY, GT)]
            before = sum(1 if p == 1 else 2 for p in range(q))
            return [(a, b, before + i + 1) for i, (a, b) in enumerate(parts)]

        def ranks_bank(q):
            return bank[5 if q == GROUPS else 7]

        def logits_bank(q, t):
            return bank[7 if q != 1 and t >= EARLY else 6]

        MOVES = 2

        block = ctx.enter_context(nc.Block())

        @block.sync
        def _(sp):
            def load(dst, src, done):
                sp.dma_start(dst, src).then_inc(done, 16)

            def zero_slots(g):
                sp.dma_start(xs_rows[g].rearrange("(t p) d -> p t d", p=P),
                             zeros.unsqueeze(1).broadcast_to([P, SLOT_TILES, D])).then_inc(slots_zeroed[g], 16)

            load(x[:, 0:EARLY, :], x_tok[:, 0:EARLY, :], x_early_loaded)
            load(wr_sb[:], wr, wr_loaded)
            load(x[:, EARLY:GT, :], x_tok[:, EARLY:GT, :], x_loaded[0])
            load(br_all[:], br.unsqueeze(0).broadcast_to([P, E]), router_w_loaded)
            load(ws1_sb[:], ws1, router_w_loaded)
            load(ws2_sb[:], ws2, router_w_loaded)
            load(bs1_col[:], bs1.unsqueeze(1), router_w_loaded)
            load(be1_rows[:], be1, router_w_loaded)
            load(attn_rows[:, 0:3, :], qkv_w.rearrange("(c p) d -> p c d", p=P), attn_w_loaded)
            load(attn_rows[:, 3, :], out_w, attn_w_loaded)
            load(bias_row[:, 0:3 * D], qkv_b.unsqueeze(0), attn_w_loaded)
            load(bias_row[:, 3 * D:4 * D], out_b.unsqueeze(0), attn_w_loaded)
            sp.wait_ge(zeros_made, 2)
            for j in range(4):
                load(be2_aug[RP * j:RP * j + E, j, :], be2, router_w_loaded)
                load(be2_aug[RP * j + E:RP * j + RP, j, :], bs2.unsqueeze(0), router_w_loaded)
            load(x[:, GT:2 * GT, :], x_tok[:, GT:2 * GT, :], x_loaded[1])
            zero_slots(0)
            load(experts[:, :, 0:F], we1.rearrange("e d f -> d e f"), experts_loaded)
            load(experts[:, :, F:2 * F], we2.rearrange("e f d -> f e d"), experts_loaded)
            zero_slots(1)

            def load_slots(q):
                g = q % GROUPS
                sp.wait_ge(xs_scattered[g], 16 * GT * TOPK * (q // GROUPS + 1))

                def load_chunk(C, i):
                    wait_chunks(sp, xs_transposed, C - RING + 1, i)
                    sp.dma_start(xs_in[:, C % RING, :, :], of_chunk(xs_chunks[g], C - q * CHUNKS, i)
                                 ).then_inc(xs_loaded[C % RING], 16)

                def step(C, i, head, tail):
                    if head:
                        load_chunk(C, i)
                        load_chunk(C + 1, i)
                    if C + 2 < (q + 1) * CHUNKS:
                        load_chunk(C + 2, i)

                chunk_steps(sp, q, step)

            for q in range(2 * GROUPS):
                load_slots(q)
                if q == 1:
                    sp.wait_ge(bias_split, 1)
                    load(bias3[:], bias_parts[:], bias_loaded)
            parts = [(4 * j, 4 * j + 4) for j in range(TILES // 4 - 1)] + [(t, t + 1) for t in range(TILES - 4, TILES)]
            for i, (a, b) in enumerate(parts):
                sp.wait_ge(x_final, i + 1)
                sp.dma_start(out_tok[:, a:b, :], x[:, a:b, :]).then_inc(out_stored, 16)
            sp.wait_ge(out_stored, 16 * len(parts))

        @block.gpsimd
        def _(pool):
            pool.memset(be2_aug[:], 0.0).then_inc(zeros_made, 1)
            pool.memset(zeros, 0.0).then_inc(zeros_made, 1)
            made = [0]

            def link(ins):
                made[0] += 1
                ins.then_inc(pool_step, 1)
                pool.wait_ge(pool_step, made[0])

            pool.memset(ident[:], 0.0)
            pool.memset(tri[:], 1.0)
            pool.memset(before[:], 1.0)
            pool.memset(ones[:], 1.0)
            pool.memset(head_mask[:], 1.0)
            pool.memset(zero_row[:], 0.0)
            pool.memset(v_aug[:], 1.0)
            pool.memset(gates[:], 1.0)
            pool.iota(expert_ids[:], [[1, E]], base=0, channel_multiplier=0, allow_small_or_imprecise_dtypes=True)
            link(pool.iota(row_id[:], [[1, 1]], base=0, channel_multiplier=1, allow_small_or_imprecise_dtypes=True))
            pool.affine_select(out=ident[:], in_=ident[:], compare_op=ALU.not_equal, fill=1.0, base=0,
                               pattern=[[-1, P]], channel_multiplier=1)
            pool.affine_select(out=tri[:], in_=tri[:], compare_op=ALU.is_ge, fill=0.0, base=0,
                               pattern=[[1, P]], channel_multiplier=-1)
            pool.affine_select(out=before[:], in_=before[:], compare_op=ALU.is_ge, fill=0.0, base=-1,
                               pattern=[[1, P]], channel_multiplier=-1)
            link(pool.affine_select(out=head_mask[:], in_=head_mask[:], compare_op=ALU.is_ge, fill=0.0, base=0,
                                    pattern=[[-HD, HEADS], [0, HA]], channel_multiplier=1))
            pool.affine_select(out=head_mask[:], in_=head_mask[:], compare_op=ALU.is_ge, fill=0.0, base=HD - 1,
                               pattern=[[HD, HEADS], [0, HA]], channel_multiplier=-1).then_inc(consts_made, 1)

            def scatter(q, row):
                g, t, k = q % GROUPS, row // TOPK, row % TOPK
                if row == 0:
                    pool.wait_ge(slots_zeroed[g], 16)
                for i, (a, b) in enumerate(SLOT_PARTS):
                    if row == TOPK * a:
                        pool.wait_ge(slots_ready, len(SLOT_PARTS) * q + i + 1)
                n = g * GT + t
                pool.indirect_dma_start(xs_rows[g], bass.IndirectOffsetOnAxis(slots[:, n, k:k + 1], 0),
                                        xn[:, n, :], None).then_inc(xs_scattered[g], 16)

            def gather(q, row):
                g, t, k = q % GROUPS, row // TOPK, row % TOPK
                if row == 0:
                    for r, n in enumerate(stored_before((q + 1) * CHUNKS)):
                        pool.wait_ge(ys_stored[r], 16 * n)
                n = q * QUADS + t // 4
                if row % (4 * TOPK) == 0 and n >= 2:
                    pool.wait_ge(y_gathered[n % 2], 16 * 4 * TOPK * (n // 2))
                pool.indirect_dma_start(y_tok[:, g * GT + t, k, :], None, ys_rows[g],
                                        bass.IndirectOffsetOnAxis(slots[:, g * GT + t, k:k + 1], 0)
                                        ).then_inc(y_gathered_last[t % 4] if n == 2 * TILES // 4 - 1
                                                   else y_gathered[n % 2], 16)

            def outer(n):
                pool.wait_ge(features_ready, n + 1)
                if n >= 2:
                    pool.wait_ge(sums_done, CUTS * (n - 1))
                k = qk[:, n % 2, D:2 * D].rearrange("p (h d) -> p h d", h=HEADS)
                pool.tensor_tensor(kv[:, n % 2, :, :, :], k.unsqueeze(2).broadcast_to([P, HEADS, HA, HD]),
                                   v_aug[:, n % 2, :, :].unsqueeze(3).broadcast_to([P, HEADS, HA, HD]), ALU.mult
                                   ).then_inc(kv_ready, 1)

            ROWS = GT * TOPK
            for move, q in ((scatter, 0), (scatter, 1), (gather, 0)):
                for row in range(ROWS):
                    move(q, row)
            for g, move, q in ((0, gather, 1), (1, scatter, GROUPS)):
                for t in range(GT):
                    outer(g * GT + t)
                    for row in range(MOVES * t, MOVES * t + MOVES):
                        move(q, row)
                for row in range(MOVES * GT, ROWS):
                    move(q, row)
            for move, q in ((scatter, GROUPS + 1), (gather, GROUPS), (gather, GROUPS + 1)):
                for row in range(ROWS):
                    move(q, row)

        @block.scalar
        def _(act):
            def copy(dst, src):
                return act.activation(dst, src, ACT.Copy)

            def normed(g, j):
                n = g * QUADS + j
                act.wait_ge(norm_ready, n + 1)
                if n >= 1:
                    act.wait_ge(xa_transposed, n)
                for i in range(4):
                    ins = act.activation(xa[:, i, :], x[:, g * GT + 4 * j + i, :], ACT.Identity,
                                         bias=shift4[:, i:i + 1], scale=rstd4[:, i:i + 1])
                ins.then_inc(xa_ready, 1)

            def turned(g, j):
                n = g * QUADS + j
                act.wait_ge(xa_transposed, n + 1)
                if n == 0:
                    for r in range(RING):
                        act.wait_ge(ys_stored[r], 16 * stored_before(GROUPS * CHUNKS)[r])
                copy(xaT[:, n % 2, :], bank[0][:]).then_inc(xaT_ready, 1)

            def features(g, t):
                n = g * GT + t
                act.wait_ge(qkv_done, n + 1)
                if n >= 2:
                    act.wait_ge(sums_read, CUTS * (n - 1))
                    act.wait_ge(state_done, n - 1)
                act.activation(qk_relu[:], bank[1][:, 0:2 * D], ACT.Relu).then_inc(relu_done, 1)
                copy(v_aug[:, n % 2, :, 0:HD],
                     bank[1][:, 2 * D:3 * D].rearrange("p (h e) -> p h e", h=HEADS))
                act.wait_ge(relu_done, n + 1)
                act.activation(qk[:, n % 2, :], qk_relu[:], ACT.Copy, bias=FEATURE_EPS
                               ).then_inc(features_ready, 1)

            def group_rows(q, j, rows):
                for t in [4 * j + i for i in rows]:
                    n = (q % GROUPS) * GT + t
                    ins = act.activation(xn[:, n, :], x[:, n, :], ACT.Identity,
                                         bias=group_norm[8][:, t:t + 1], scale=group_norm[3][:, t:t + 1])
                return ins

            def exponents(lo, hi, n):
                act.wait_ge(exp_asked, n)
                act.activation(probs[:, lo:hi, 0:E], logits[:, lo:hi, 0:E], ACT.Exp).then_inc(exp_done, 1)

            def group_turned(q, j):
                act.wait_ge(xn_transposed, q * QUADS + j + 1)
                copy(xnT[:, 512 * j:512 * j + 512], xnT_bank(q, j)[:]).then_inc(xnT_ready, 1)

            def route(q):
                g = q % GROUPS
                if q == 0:
                    act.wait_ge(group_norm_ready, norm_count(q, early=True))
                    for j in range(EARLY_QUADS):
                        if normed_by_act(q, j):
                            group_rows(q, j, range(4)).then_inc(xn_ready_act, 1)
                    for j in range(EARLY_QUADS):
                        group_turned(q, j)
                act.wait_ge(group_norm_ready, norm_count(q))
                if q >= GROUPS:
                    act.wait_ge(xs_scattered[g], 16 * GT * TOPK * (q // GROUPS))
                early = 0 if q == 1 else EARLY_QUADS
                for j in range(early, QUADS):
                    if normed_by_act(q, j):
                        group_rows(q, j, range(4)).then_inc(xn_ready_act, 1)
                for j in range(early, QUADS):
                    group_turned(q, j)
                    if q != 1 and j == EARLY_QUADS:
                        exponents(*softmax_parts(q)[0])
                if q == 0:
                    act.wait_ge(w_transposed, 1)
                    copy(attn_wT[:], bank[2][:].rearrange("p (c d) -> p c d", c=4)).then_inc(consts_made, 1)
                exponents(*softmax_parts(q)[-1])
                if q == GROUPS:
                    normed(1, 0)
                    turned(1, 0)
                    features(1, 0)

            def shared(q):
                n = shared_before(q)
                if q == GROUPS:
                    for j in range(QUADS):
                        group_turned(TURN_AGAIN, j)
                for j in range(QUADS):
                    act.wait_ge(shared_h_done, n * QUADS + j + 1)
                    act.activation(sharedT[:, 512 * j:512 * j + 512], bank[j % 2][:], ACT.Gelu,
                                   bias=bs1_col[:]).then_inc(sharedT_ready, 1)
                act.wait_ge(gates_transposed, n + 1)
                copy(gatesT[:].rearrange("p j t -> p (j t)"), bank[0][:]).then_inc(gatesT_ready, 1)

            def run_experts(q):
                g = q % GROUPS

                def store(C, i):
                    wait_chunks(act, ys_ready, C + 1, i)
                    act.dma_start(of_chunk(ys_chunks[g], C - q * CHUNKS, i), ys_out[:, C % RING, :, :]
                                  ).then_inc(ys_stored[C % RING], 16)

                def results(C, i):
                    wait_chunks(act, y_done, C + 1, i)
                    if C >= RING:
                        act.wait_ge(ys_stored[C % RING], 16 * (C // RING) + (i * 16 if not isinstance(i, int) else 0))
                    elif not isinstance(i, int):
                        act.wait_ge(ys_stored[C % RING], i * 16)
                    copy(ys_out[:, C % RING, :, :].rearrange("p u d -> p (u d)"),
                                    bank[4 + C % 2][:, 0:CH * P]).then_inc(ys_ready, 1)

                def step(C, i, head, tail):
                    wait_chunks(act, h_done, C + 1, i)
                    wait_chunks(act, y_done, C - 1, i)
                    for u in range(CH):
                        ins = act.activation(hT[:, C % 2, u * P:(u + 1) * P], bank[2 + C % 2][:, u * P:(u + 1) * P],
                                             ACT.Gelu, bias=w_ring[:, C % RING, u, 2 * F:2 * F + 1])
                    ins.then_inc(hT_ready, 1)
                    if not head:
                        results(C - 1, i)
                    if C - q * CHUNKS >= 2:
                        store(C - 2, i)
                    if tail:
                        store(C - 1, i)
                        results(C, i)
                        store(C, i)

                chunk_steps(act, q, step)

            def attend(g):
                first = g * GT

                def transposed(t):
                    n = g * (GT + 1) + t
                    act.wait_ge(q_o_transposed, n + 1)
                    lo, hi = (0, 1) if t == 0 else (1, 2) if t == GT else (0, 2)
                    copy(q_oT[:, lo:hi, :], bank[7][:, lo * P:hi * P].rearrange("p (c t) -> p c t", t=P)
                         ).then_inc(q_oT_ready, 1)

                def attended(t):
                    act.wait_ge(projected, first + t + 1)
                    copy(x[:, first + t, :], bank[7][:, 2 * P:3 * P]).then_inc(x_attended, 1)

                def early_rows(k):
                    q = GROUPS + g
                    if 0 <= k < 2 * EARLY_QUADS:
                        if k == 0:
                            act.wait_ge(group_norm_ready, norm_count(q, early=True))
                            act.wait_ge(xs_scattered[g], 16 * GT * TOPK)
                        ins = group_rows(q, k // 2, (2 * (k % 2), 2 * (k % 2) + 1))
                        if k % 2:
                            ins.then_inc(xn_ready_act, 1)
                    if k >= 3 and k % 2:
                        group_turned(q, k // 2 - 1)

                if g == 0:
                    normed(0, 0)
                    turned(0, 0)
                    features(0, 0)
                transposed(0)
                if g == 0:
                    act.activation(exp_table[:], row_id[:], ACT.Exp, scale=0.0)
                features(g, 1)
                for t in range(GT):
                    if t % 4 == 1 and t + 3 < GT:
                        turned(g, t // 4 + 1)
                    if t + 2 < GT:
                        features(g, t + 2)
                    transposed(t + 1)
                    if t % 4 == 0 and t + 4 < GT:
                        normed(g, t // 4 + 1)
                    attended(t)
                    early_rows(t - GT + 2 * EARLY_QUADS)
                early_rows(2 * EARLY_QUADS + 1)

            for q in range(GROUPS):
                route(q)
                shared(q)
            run_experts(0)
            run_experts(1)
            for g in range(GROUPS):
                attend(g)
                route(GROUPS + g)
            run_experts(2)
            run_experts(3)
            shared(3)
            shared(2)

        @block.tensor
        def _(pe):
            pe.wait_ge(consts_made, 1)

            def quad(g, j):
                n = g * QUADS + j
                pe.wait_ge(xa_ready, n + 1)
                if n >= 1:
                    pe.wait_ge(xaT_ready, n)
                for i in range(4):
                    ins = pe.transpose(bank[0][:, i * P:(i + 1) * P], xa[:, i, :], ident[:])
                ins.then_inc(xa_transposed, 1)

            def project(g, t):
                n = g * GT + t
                if t % 4 == 0:
                    pe.wait_ge(xaT_ready, n // 4 + 1)
                if n >= 1:
                    pe.wait_ge(features_ready, n)
                o = bank[1][:, 0:3 * D]
                pe.matmul(o, xaT[:, (n // 4) % 2, (t % 4) * P:(t % 4 + 1) * P],
                          attn_wT[:, 0:3, :].rearrange("p c d -> p (c d)"), start=True, stop=False)
                pe.matmul(o, ones[0:3, :], bias3[:, 0:3 * D], start=False, stop=True).then_inc(qkv_done, 1)

            def turn_group(q, j):
                if q < TURN_AGAIN:
                    pe.wait_ge(xn_ready_act if normed_by_act(q, j) else xn_ready, xn_count(q, j))
                if q == TURN_AGAIN:
                    if j < 2:
                        pe.wait_ge(gatesT_ready, shared_before(GROUPS))
                    else:
                        pe.wait_ge(xnT_ready, q * QUADS + j - 1)
                elif q >= GROUPS and j == 0:
                    pe.wait_ge(xaT_ready, (q - GROUPS + 1) * QUADS)
                elif q >= GROUPS:
                    pe.wait_ge(xnT_ready, q * QUADS + min(j, EARLY_QUADS))
                elif q * QUADS + j >= 2:
                    pe.wait_ge(xnT_ready, q * QUADS + j - 1)
                for i in range(4):
                    ins = pe.transpose(xnT_bank(q, j)[:, i * P:(i + 1) * P],
                                       xn[:, (q % GROUPS) * GT + 4 * j + i, :], ident[:])
                ins.then_inc(xn_transposed, 1)

            def route(q):
                g = q % GROUPS

                def group_logits(a, b):
                    for t in range(a, b):
                        if t % 4 == 0:
                            pe.wait_ge(xnT_ready, q * QUADS + t // 4 + 1)
                        ins = pe.matmul(logits_bank(q, t)[:, t * RP:t * RP + E], xnT[:, t * P:(t + 1) * P],
                                        wr_sb[:], start=True, stop=True)
                    return ins

                early = 0 if q == 1 else EARLY_QUADS
                if q == 0:
                    for j in range(EARLY_QUADS):
                        turn_group(q, j)
                    pe.wait_ge(wr_loaded, 16)
                if q >= GROUPS:
                    pe.wait_ge(carried_read, (g + 1) * (GT - GT // BT))
                if q != 1:
                    group_logits(0, EARLY).then_inc(logits_done, 1)
                for j in range(early, QUADS):
                    turn_group(q, j)
                ins = group_logits(4 * early, GT)
                ins.then_inc(logits_done, 1)
                if q == 0:
                    pe.wait_ge(attn_w_loaded, 16 * N_ATTN_W)
                    pe.wait_ge(router_w_loaded, 16 * N_ROUTER_W)
                    pe.transpose(bank[3][:, 0:E], be1_rows[:], ident[0:E, 0:E])
                    for c in range(4):
                        ins = pe.transpose(bank[2][:, c * P:(c + 1) * P], attn_rows[:, c, :], ident[:])
                    ins.then_inc(w_transposed, 1)
                if q < GROUPS:
                    shared_first(q)
                if q == GROUPS:
                    quad(1, 0)
                    project(1, 0)
                pe.wait_ge(chosen_ready, q + 1)
                for t in range(GT):
                    ins = pe.matmul(bank[6][:, 0:E], ones[:], chosen[:, t, :], start=t == 0, stop=t == GT - 1)
                ins.then_inc(counts_done, 1)
                o = ranks_bank(q)
                pe.matmul(o[:, 0:GT * E], before[:], chosen[:].rearrange("p t e -> p (t e)"),
                          start=True, stop=False, skip_group_check=True)
                for s in range(1, GT):
                    ins = pe.matmul(o[:, s * E:GT * E], ones[:],
                                    chosen[:, 0:GT - s, :].rearrange("p t e -> p (t e)"),
                                    start=False, stop=s == GT - 1, skip_group_check=True)
                ins.then_inc(ranks_done, 1)
                pe.wait_ge(tile_expert_ready, q + 1)
                pe.matmul(bank[6][0:1, P:2 * P], tile_expert[:], ident[:], start=True, stop=True
                          ).then_inc(expert_row_done, 1)

            def shared_h(q, j):
                n = shared_before(q) * QUADS + j
                if j >= 2:
                    pe.wait_ge(sharedT_ready, n - 1)
                pe.matmul(bank[j % 2][:], ws1_sb[:], xnT[:, 512 * j:512 * j + 512],
                          start=True, stop=True).then_inc(shared_h_done, 1)

            def shared_out(q, j):
                pe.wait_ge(sharedT_ready, shared_before(q) * QUADS + j + 1)
                for i in range(4):
                    t = 4 * j + i
                    pe.matmul(bank[2 + j][:, i * P:(i + 1) * P], sharedT[:, t * P:(t + 1) * P], ws2_sb[:],
                              start=i == 0, stop=False, skip_group_check=True)

            def shared_first(q):
                shared_h(q, 0)
                shared_h(q, 1)
                if q == 0:
                    pe.wait_ge(consts_made, 3)
                else:
                    pe.wait_ge(shared_out_read, shared_before(q) * QUADS)
                for j in range(QUADS - 2):
                    shared_h(q, j + 2)
                    shared_out(q, j)

            def shared_rest(q):
                n = shared_before(q)
                for j in range(QUADS - 2, QUADS):
                    shared_out(q, j)
                pe.wait_ge(gates_ready, q + 1)
                pe.wait_ge(sharedT_ready, (n + 1) * QUADS)
                for j in range(QUADS):
                    ins = pe.transpose(bank[0][:, j * P:(j + 1) * P],
                                       gates[:, q % GROUPS, 4 * j:4 * j + 4, :].rearrange("p t e -> p (t e)"),
                                       ident[:])
                ins.then_inc(gates_transposed, 1)
                pe.wait_ge(gatesT_ready, n + 1)
                for j in range(QUADS):
                    for i in range(4):
                        ins = pe.matmul(bank[2 + j][:, i * P:(i + 1) * P], gatesT[:, j, :], be2_aug[:, i, :],
                                        start=False, stop=True, skip_group_check=True)
                    ins.then_inc(shared_out_done, 1)

            def shared(q):
                if shared_before(q) == GROUPS:
                    pe.wait_ge(xsT_ready, 2 * GROUPS * CHUNKS)
                    pe.wait_ge(hT_ready, 2 * GROUPS * CHUNKS)
                    pe.wait_ge(ys_ready, 2 * GROUPS * CHUNKS)
                if q == GROUPS:
                    for j in range(QUADS):
                        turn_group(TURN_AGAIN, j)
                    pe.wait_ge(xnT_ready, (TURN_AGAIN + 1) * QUADS)
                shared_first(q)
                shared_rest(q)

            def run_experts(q):
                pe.wait_ge(shared_out_read, QUADS * GROUPS)
                if q >= GROUPS:
                    pe.wait_ge(sums_read, CUTS * TILES)

                def transposes(C, i):
                    r = C % RING
                    pe.wait_ge(xs_loaded[r], 16 * (C // RING + 1) + (i * 16 if not isinstance(i, int) else 0))
                    wait_chunks(pe, xsT_ready, C - 1, i)
                    for u in range(CH):
                        ins = pe.transpose(bank[C % 2][:, u * P:(u + 1) * P], xs_in[:, r, u, :], ident[:])
                    ins.then_inc(xs_transposed, 1)

                def down(C, i):
                    wait_chunks(pe, hT_ready, C + 1, i)
                    wait_chunks(pe, ys_ready, C - 1, i)
                    for u in range(CH):
                        ins = pe.matmul(bank[4 + C % 2][:, u * P:(u + 1) * P], hT[:, C % 2, u * P:(u + 1) * P],
                                        w_ring[:, C % RING, u, F:2 * F], start=True, stop=True)
                    ins.then_inc(y_done, 1)

                def step(C, i, head, tail):
                    if head:
                        transposes(C, i)
                    if not tail:
                        transposes(C + 1, i)
                    wait_chunks(pe, xsT_ready, C + 1, i)
                    wait_chunks(pe, weights_copied, C + 1, i)
                    wait_chunks(pe, hT_ready, C - 1, i)
                    for u in range(CH):
                        ins = pe.matmul(bank[2 + C % 2][:, u * P:(u + 1) * P], w_ring[:, C % RING, u, 0:F],
                                        xsT[:, C % 2, u * P:(u + 1) * P], start=True, stop=True)
                    ins.then_inc(h_done, 1)
                    if not head:
                        down(C - 1, i)
                    if tail:
                        down(C, i)

                chunk_steps(pe, q, step)

            def attend(g):
                first = g * GT
                burst0 = g * (GT + 1)

                def running_sums(t):
                    n = first + t
                    pe.wait_ge(kv_ready, n + 1)
                    for c, (a, b) in enumerate(HEAD_CUTS):
                        if n == 0:
                            pe.wait_ge(shared_out_read, QUADS * (GROUPS - 1) + c + 1)
                        if n >= 1:
                            pe.wait_ge(sums_read, CUTS * (n - 1) + c + 1)
                        pe.matmul(bank[2 + c][:, 0:(b - a) * HA * HD], tri[:],
                                  kv[:, n % 2, a:b, :, :].rearrange("p h e d -> p (h e d)"),
                                  start=True, stop=True).then_inc(sums_done, 1)
                    if n >= 1:
                        pe.wait_ge(state_ready, n - n // BT)
                    if n == 0:
                        pe.wait_ge(shared_out_read, QUADS * GROUPS)
                    if n == GT:
                        pe.wait_ge(slots_ready, len(SLOT_PARTS) * (GROUPS + 1))
                    pe.matmul(bank[5][:, 0:HEADS * HA], qk[:, n % 2, D:2 * D],
                              v_aug[:, n % 2, :, :].rearrange("p h e -> p (h e)"), start=t % BT == 0,
                              stop=True, skip_group_check=True).then_inc(state_done, 1)

                def burst(t):
                    n = burst0 + t
                    if t > 0:
                        pe.wait_ge(attn_o_ready, first + t)
                    if n >= 1:
                        pe.wait_ge(x_attended, first + max(t - 1, 0))
                        pe.wait_ge(q_oT_ready, n)
                    if t < GT:
                        pe.wait_ge(features_ready, first + t + 1)
                        ins = pe.transpose(bank[7][:, 0:P], qk[:, (first + t) % 2, 0:D], ident[:])
                    if t > 0:
                        ins = pe.transpose(bank[7][:, P:2 * P], attn_o[:], ident[:])
                    ins.then_inc(q_o_transposed, 1)
                    if 1 <= t < GT - 2:
                        project(g, t + 2)
                    pe.wait_ge(q_oT_ready, n + 1)
                    if t % BT and t < GT:
                        done = (first + t) - (first + t) // BT
                        pe.wait_ge(state_ready, done)
                        if done > 1:
                            pe.wait_ge(carried_read, done - 1)
                        pe.matmul(bank[6][:, 0:HEADS * HA], q_oT[:, 0, :], state[:], start=True, stop=True
                                  ).then_inc(carried_done, 1)
                    if t > 0:
                        o = bank[7][:, 2 * P:3 * P]
                        pe.matmul(o, q_oT[:, 1, :], attn_wT[:, 3, :], start=True, stop=False)
                        pe.matmul(o, ones[0:3, :], bias3[:, 3 * D:4 * D], start=False, stop=False)
                        pe.matmul(o, ident[:], x[:, first + t - 1, :], start=False, stop=True).then_inc(projected, 1)

                if g == 0:
                    pe.wait_ge(bias_loaded, 16)
                    quad(0, 0)
                    project(0, 0)
                    pe.wait_ge(slots_ready, len(SLOT_PARTS) * GROUPS)
                burst(0)
                project(g, 1)
                running_sums(0)
                project(g, 2)
                for t in range(GT):
                    if t % 4 == 1 and t + 3 < GT:
                        quad(g, t // 4 + 1)
                    if t + 1 < GT:
                        running_sums(t + 1)
                    burst(t + 1)
                    k = t - GT + 2 * EARLY_QUADS
                    if k > 0 and k % 2 == 0:
                        turn_group(GROUPS + g, k // 2 - 1)
                turn_group(GROUPS + g, EARLY_QUADS - 1)

            for q in range(GROUPS):
                route(q)
                shared_rest(q)
            run_experts(0)
            run_experts(1)
            for g in range(GROUPS):
                attend(g)
                route(GROUPS + g)
            run_experts(2)
            run_experts(3)
            shared(3)
            shared(2)

        @block.vector
        def _(dve):
            steps = [0]

            def link(ins):
                steps[0] += 1
                ins.then_inc(dve_step, 1)
                dve.wait_ge(dve_step, steps[0])

            NORM_STAGES = 17
            STATS_LAG = 2

            def norm_stage(k, first, lo, hi, bufs):
                m, v, r, a, b, bits, f, sh = (buf[:, lo:hi] for buf in bufs[1:])
                s, y0 = bufs[0][:, lo:hi, :], bits.bitcast(F32)
                if k == 0:
                    for t in range(hi - lo):
                        ins = dve.bn_stats(s[:, t, :], x[:, first + lo + t, :])
                elif k == 1:
                    dve.tensor_tensor(a, s[:, :, 1], s[:, :, 4], ALU.subtract)
                    dve.tensor_tensor(b, s[:, :, 2], s[:, :, 5], ALU.add)
                    ins = dve.tensor_tensor(r, s[:, :, 1], s[:, :, 4], ALU.add)
                elif k == 2:
                    dve.tensor_scalar(m, r, 0.5, None, ALU.mult)
                    dve.tensor_scalar(v, b, 1.0 / D, LN_EPS, ALU.mult, ALU.add)
                    ins = dve.scalar_tensor_tensor(out=f, in0=a, scalar=0.25, in1=a,
                                                   op0=ALU.mult, op1=ALU.mult)
                elif k == 3:
                    ins = dve.tensor_tensor(v, v, f, ALU.add)
                elif k == 4:
                    ins = dve.tensor_scalar(bits, v.bitcast(I32), 1, None, ALU.logical_shift_right)
                elif k == 5:
                    ins = dve.tensor_copy(f, bits)
                elif k == 6:
                    ins = dve.tensor_scalar(bits, f, -1.0, float(RSQRT_SEED), ALU.mult, ALU.add)
                elif k < 16:
                    y = y0 if k < 10 else r
                    if (k - 7) % 3 == 0:
                        ins = dve.tensor_tensor(a, y, y, ALU.mult)
                    elif (k - 7) % 3 == 1:
                        ins = dve.scalar_tensor_tensor(out=b, in0=a, scalar=-0.5, in1=v, op0=ALU.mult, op1=ALU.mult)
                    else:
                        ins = dve.scalar_tensor_tensor(out=r, in0=b, scalar=1.5, in1=y, op0=ALU.add, op1=ALU.mult)
                else:
                    ins = dve.scalar_tensor_tensor(out=sh, in0=m, scalar=-1.0, in1=r,
                                                   op0=ALU.mult, op1=ALU.mult)
                return ins

            def over_tiles(a):
                return a.unsqueeze(1).broadcast_to([P, GT, E])

            def group_norms(q, lo, hi, last):
                for k in range(1, NORM_STAGES):
                    ins = norm_stage(k, (q % GROUPS) * GT, lo, hi, group_norm)
                    if k == NORM_STAGES - 1:
                        ins.then_inc(group_norm_ready, 1)
                        dve.wait_ge(group_norm_ready, norm_count(q, early=not last))
                    else:
                        link(ins)

            def group_rows(q, a, b):
                first = (q % GROUPS) * GT
                for j in range(a, b):
                    if normed_by_act(q, j):
                        continue
                    for t in range(4 * j, 4 * j + 4):
                        ins = dve.tensor_scalar(xn[:, first + t, :], x[:, first + t, :], group_norm[1][:, t:t + 1],
                                                group_norm[3][:, t:t + 1], ALU.subtract, ALU.mult)
                    ins.then_inc(xn_ready, 1)

            def group_stats(q):
                first = (q % GROUPS) * GT
                if q == 0:
                    dve.wait_ge(x_early_loaded, 16)
                    link(norm_stage(0, first, 0, EARLY, group_norm))
                    group_norms(q, 0, EARLY, False)
                    group_rows(q, 0, EARLY_QUADS)
                    dve.wait_ge(x_loaded[0], 16)
                    link(norm_stage(0, first, EARLY, GT, group_norm))
                    group_norms(q, EARLY, GT, True)
                elif q == 1:
                    dve.wait_ge(x_loaded[1], 16)
                    dve.wait_ge(xn_ready_act, xn_count(0, QUADS - 1))
                    link(norm_stage(0, first, 0, GT, group_norm))
                    group_norms(q, 0, GT, True)
                else:
                    fill(q)
                    fill(q)
                    dve.wait_ge(x_attended, first + GT)
                    link(norm_stage(0, first, GT - STATS_LAG, GT, group_norm))
                    group_norms(q, EARLY, GT, True)

            QUADS_AHEAD = 19
            ahead = [0]

            def fill(q):
                if q == GROUPS and ahead[0] < QUADS_AHEAD:
                    quad_stage(1, 1, ahead[0])
                    ahead[0] += 1

            def link_filled(q, ins):
                landed = mark(ins)
                fill(q)
                dve.wait_ge(dve_step, landed)

            def softmax(q, lo, hi, n):
                def link(ins):
                    link_filled(q, ins)

                def per_tile(a):
                    return a.unsqueeze(2).broadcast_to([P, hi - lo, E])

                lg, pr = logits[:, lo:hi, 0:E], probs[:, lo:hi, 0:E]
                raw = logits_bank(q, lo)[:].rearrange("p (t e) -> p t e", e=RP)[:, lo:hi, 0:E]
                dve.wait_ge(logits_done, n)
                link(dve.tensor_tensor(lg, raw, br_all[:].unsqueeze(1).broadcast_to([P, hi - lo, E]), ALU.add))
                link(dve.tensor_reduce(row_max[:, lo:hi], lg, AXX, ALU.max))
                dve.tensor_tensor(lg, lg, per_tile(row_max[:, lo:hi]), ALU.subtract).then_inc(exp_asked, 1)
                if q == 0 and hi == GT:
                    dve.wait_ge(w_transposed, 1)
                    dve.tensor_copy(experts[:, :, 2 * F], bank[3][:, 0:E]).then_inc(consts_made, 1)
                dve.wait_ge(exp_done, n)
                link(dve.tensor_reduce(row_sum[:, lo:hi], pr, AXX, ALU.add))
                link(dve.reciprocal(row_sum[:, lo:hi], row_sum[:, lo:hi]))
                link(dve.tensor_tensor(pr, pr, per_tile(row_sum[:, lo:hi]), ALU.mult))
                for t in range(lo, hi):
                    ins = dve.max(top[:, t, :], probs[:, t, 0:E])
                link(ins)
                for t in range(lo, hi):
                    ins = dve.max_index(top_id[:, t, :], top[:, t, :], probs[:, t, 0:E])
                first = (q % GROUPS) * GT
                link(dve.tensor_scalar(half_gate[:, first + lo:first + hi, :], top[:, lo:hi, 0:TOPK], 0.5, None,
                                       ALU.mult))
                link(dve.tensor_copy(top_idf[:, lo:hi, :], top_id[:, lo:hi, 0:TOPK]))
                link(dve.tensor_tensor(one_hot[:, lo:hi, :, :],
                                       top_idf[:, lo:hi, :].unsqueeze(3).broadcast_to([P, hi - lo, TOPK, E]),
                                       expert_ids[:].unsqueeze(1).unsqueeze(1).broadcast_to([P, hi - lo, TOPK, E]),
                                       ALU.is_equal))

            def route(q):
                g = q % GROUPS
                first = g * GT

                def link(ins):
                    link_filled(q, ins)

                group_stats(q)
                if q >= GROUPS:
                    dve.wait_ge(xs_scattered[g], 16 * GT * TOPK * (q // GROUPS))
                group_rows(q, 0 if q == 1 else EARLY_QUADS, QUADS)

                fill(q)
                fill(q)
                if q == 0:
                    dve.wait_ge(router_w_loaded, 16 * N_ROUTER_W)
                for part in softmax_parts(q):
                    softmax(q, *part)
                link(dve.tensor_tensor(chosen_a[:], one_hot[:, :, 0, :], one_hot[:, :, 1, :], ALU.add))
                dve.tensor_tensor(chosen[:], chosen_a[:], one_hot[:, :, 2, :], ALU.add).then_inc(chosen_ready, 1)
                dve.wait_ge(chosen_ready, q + 1)
                dve.tensor_tensor(gates[:, g, :, 0:E], probs[:, :, 0:E], chosen[:], ALU.mult).then_inc(gates_ready, 1)
                dve.wait_ge(counts_done, q + 1)
                link(dve.tensor_scalar(count_i[:], bank[6][:, 0:E], float(P - 1), None, ALU.add))
                link(dve.tensor_scalar(count_t[:], count_i[:], 7, None, ALU.logical_shift_right))
                link(dve.tensor_copy(run_tiles[:], count_t[:]))
                link(dve.tensor_tensor_scan(run_end[:], run_tiles[:], zero_row[:], 0.0, ALU.add, ALU.add))
                dve.tensor_scalar(ended[:], run_end[:], row_id[:, 0:1], None, ALU.is_le)
                link(dve.tensor_tensor(run_base[:], run_end[:], run_tiles[:], ALU.subtract))
                link(dve.tensor_reduce(tile_expert[:], ended[:], AXX, ALU.add))
                dve.tensor_scalar(tile_expert[:], tile_expert[:], float(E - 1), None, ALU.min
                                  ).then_inc(tile_expert_ready, 1)
                link(dve.tensor_scalar(run_base[:], run_base[:], float(P), None, ALU.mult))
                dve.wait_ge(ranks_done, q + 1)
                for a, b in SLOT_PARTS:
                    link(dve.tensor_tensor(slot_of[:, a:b, :],
                                           ranks_bank(q)[:, a * E:b * E].rearrange("p (t e) -> p t e", e=E),
                                           run_base[:].unsqueeze(1).broadcast_to([P, b - a, E]), ALU.add))
                    link(dve.tensor_tensor(hot_slots[:, a:b, :, :], one_hot[:, a:b, :, :],
                                           slot_of[:, a:b, :].unsqueeze(2).broadcast_to([P, b - a, TOPK, E]),
                                           ALU.mult))
                    link(dve.tensor_reduce(slot_f[:, a:b, :], hot_slots[:, a:b, :, :], AXX, ALU.add))
                    dve.tensor_copy(slots[:, first + a:first + b, :], slot_f[:, a:b, :]).then_inc(slots_ready, 1)
                dve.wait_ge(expert_row_done, q + 1)
                link(dve.tensor_copy(expert_tab[0:1, g * P:g * P + P], bank[6][0:1, P:2 * P]))

            def shared(q):
                first = (q % GROUPS) * GT
                n = shared_before(q)
                dve.wait_ge(xn_ready, xn_count(q, QUADS - 2))
                dve.wait_ge(xn_ready_act, xn_count(q, QUADS - 1))
                xg = x[:, first:first + GT, :]
                dve.scalar_tensor_tensor(out=xg, in0=xn[:, first:first + GT, :], scalar=0.5, in1=xg,
                                         op0=ALU.mult, op1=ALU.add).then_inc(normed_added, 1)
                dve.wait_ge(normed_added, n + 1)
                for j in range(QUADS):
                    dve.wait_ge(shared_out_done, n * QUADS + j + 1)
                    xq = x[:, first + 4 * j:first + 4 * j + 4, :].rearrange("p t d -> p (t d)")
                    dve.scalar_tensor_tensor(out=xq, in0=bank[2 + j][:], scalar=0.5, in1=xq,
                                             op0=ALU.mult, op1=ALU.add).then_inc(shared_out_read, 1)
                dve.wait_ge(shared_out_read, QUADS * (n + 1))

            def split_biases():
                dve.wait_ge(attn_w_loaded, 16 * N_ATTN_W)
                for k in range(3):
                    ins = dve.tensor_copy(bias_parts[:, k, :], bias_row[:])
                    if k < 2:
                        link(ins)
                        link(dve.tensor_copy(bias_part[:], bias_parts[:, k, :]))
                        link(dve.tensor_tensor(bias_row[:], bias_row[:], bias_part[:], ALU.subtract))
                ins.then_inc(bias_split, 1)

            def run_experts(q):
                g = q % GROUPS

                def expert_ids_of(c, n, i):
                    at = g * P + c * CH
                    at = slice(at, at + n * CH) if isinstance(i, int) else bass.ds(i * (RING * CH) + at, n * CH)
                    _, ids = nc.values_load_multi_w_load_instructions(
                        expert_tab[0:1, at], engines=(mybir.EngineType.DVE,), min_val=0, max_val=E - 1,
                        skip_runtime_bounds_check_because="the table's values are capped at E - 1")
                    return {c + k: ids[k * CH:(k + 1) * CH] for k in range(n)}

                def weights(C, i):
                    wait_chunks(dve, y_done, C - RING + 1, i)
                    for u, e in enumerate(ids[C - q * CHUNKS]):
                        ins = dve.tensor_copy(w_ring[:, C % RING, u:u + 1, :], experts[:, bass.ds(e, 1), :])
                    ins.then_inc(weights_copied, 1)

                def turned(C, i):
                    wait_chunks(dve, xs_transposed, C + 1, i)
                    wait_chunks(dve, h_done, C - 1, i)
                    dve.tensor_copy(xsT[:, C % 2, :], bank[C % 2][:, 0:CH * P]).then_inc(xsT_ready, 1)

                ids = {}

                def step(C, i, head, tail):
                    c = C - q * CHUNKS
                    if c < 2 or (c - 2) % RING == 0:
                        a, b = (0, 2) if c == 0 else (2, 3) if c == 1 else (c + 1, min(c + 1 + RING, CHUNKS))
                        ids.update(expert_ids_of(a, b - a, i))
                    if head:
                        weights(C, i)
                        turned(C, i)
                    if not tail:
                        weights(C + 1, i)
                        turned(C + 1, i)
                    k = c - (CHUNKS - 4 * RING)
                    if q == 1 and 0 <= k < 2 * TOPK:
                        if k % 2 == 0 and k:
                            dve.wait_ge(dve_step, quad_step[0])
                        quad_step[0] = mark(add_choice(0, 0, k // 2, (2 * (k % 2), 2 * (k % 2) + 1)))
                    elif q == 1 and k >= 2 * TOPK:
                        k -= 2 * TOPK
                        for k in (TOPK,) if k == 0 else range(TOPK - 1 + 2 * k, TOPK + 1 + 2 * k):
                            if k < QUAD_STAGES:
                                quad_stage(0, 0, k)

                if q == 0:
                    dve.wait_ge(experts_loaded, 32)
                chunk_steps(dve, q, step)

            def add_tiles(q, j, k, tiles):
                for t in [(q % GROUPS) * GT + 4 * j + i for i in tiles]:
                    ins = dve.scalar_tensor_tensor(out=x[:, t, :], in0=y_tok[:, t, k, :],
                                                   scalar=half_gate[:, t, k:k + 1], in1=x[:, t, :],
                                                   op0=ALU.mult, op1=ALU.add)
                return ins

            def add_choice(q, j, k, tiles=range(4)):
                n = q * QUADS + j
                if k == 0:
                    dve.wait_ge(y_gathered[n % 2], 16 * 4 * TOPK * (n // 2 + 1))
                return add_tiles(q, j, k, tiles)

            QUAD_STAGES = TOPK + NORM_STAGES
            quad_step = [0]

            def mark(ins):
                steps[0] += 1
                ins.then_inc(dve_step, 1)
                return steps[0]

            def quad_stage(g, j, k):
                n = g * QUADS + j
                if k > 0:
                    dve.wait_ge(dve_step, quad_step[0])
                if k < TOPK:
                    ins = add_choice(g, j, k)
                else:
                    ins = norm_stage(k - TOPK, g * GT + 4 * j, 0, 4, quad_norm)
                quad_step[0] = mark(ins)
                if k == QUAD_STAGES - 1:
                    dve.wait_ge(dve_step, quad_step[0])
                    if n >= 1:
                        dve.wait_ge(xa_ready, n)
                    dve.tensor_copy(rstd4[:], quad_norm[3][:])
                    dve.tensor_copy(shift4[:], quad_norm[8][:]).then_inc(norm_ready, 1)

            def attend(g):
                first = g * GT
                early_step = [0]

                def early_stage(t, k):
                    if k == 0 and t >= STATS_LAG:
                        dve.wait_ge(x_attended, first + t - STATS_LAG + 1)
                        landed = mark(norm_stage(0, first, t - STATS_LAG, t - STATS_LAG + 1, group_norm))
                        if t - STATS_LAG < EARLY:
                            early_step[0] = landed
                    stage = 1 + 8 * (t - EARLY - STATS_LAG) + 2 * (k - 1)
                    if k > 0 and 0 < stage < NORM_STAGES:
                        for i in range(stage, stage + 2):
                            dve.wait_ge(dve_step, early_step[0])
                            if i == NORM_STAGES - 1:
                                dve.wait_ge(xn_ready_act, xn_count(GROUPS + g - 1, QUADS - 1))
                            ins = norm_stage(i, first, 0, EARLY, group_norm)
                            if i == NORM_STAGES - 1:
                                ins.then_inc(group_norm_ready, 1)
                            else:
                                early_step[0] = mark(ins)

                def gap(t, k):
                    early_stage(t, k)
                    if t == 0 and k == 0 and g == 0:
                        for i in range(QUAD_STAGES):
                            quad_stage(g, 1, i)
                    elif t == 0 and k == 4 and g == 1:
                        quad_stage(g, 1, QUADS_AHEAD)
                    elif 0 < t <= GT - 8:
                        j = (t + 3) // 4 + 1
                        if j < QUADS:
                            quad_stage(g, j, 5 * ((t + 3) % 4) + k)
                    elif g == 0 and t >= GT - 4:
                        quad_stage(1, 0, 5 * (t - GT + 4) + k)

                def apply(t):
                    n = first + t
                    qh = qk[:, n % 2, 0:D].rearrange("p (h d) -> p h d", h=HEADS)
                    for c, (a, b) in enumerate(HEAD_CUTS):
                        s = bank[2 + c][:, 0:(b - a) * HA * HD].rearrange("p (h e d) -> p h e d", e=HA, d=HD)
                        dve.wait_ge(sums_done, CUTS * n + c + 1)
                        dve.tensor_tensor(weighed[:, a:b, :, :], s,
                                          qh[:, a:b, :].unsqueeze(2).broadcast_to([P, b - a, HA, HD]), ALU.mult
                                          ).then_inc(sums_read, 1)
                    gap(t, 1)
                    dve.wait_ge(sums_read, CUTS * (n + 1))
                    summed = mark(dve.tensor_reduce(num_den[:], weighed[:], AXX, ALU.add))
                    gap(t, 2)
                    dve.wait_ge(dve_step, summed)
                    if t % BT:
                        dve.wait_ge(carried_done, n - n // BT)
                        nd = num_den[:].rearrange("p h e -> p (h e)")
                        ins = dve.tensor_tensor(nd, nd, bank[6][:, 0:HEADS * HA], ALU.add)
                        ins.then_inc(carried_read, 1)
                        gap(t, 3)
                        dve.wait_ge(carried_read, n - n // BT)
                    else:
                        gap(t, 3)
                    guarded = mark(dve.tensor_scalar(den[:], num_den[:, :, HD], DEN_EPS, None, ALU.max))
                    gap(t, 4)
                    dve.wait_ge(dve_step, guarded)
                    inverted = mark(dve.reciprocal(den_inv[:], den[:]))
                    if t % BT != BT - 1:
                        dve.wait_ge(state_done, n + 1)
                        dve.tensor_tensor(state[:], bank[5][:, 0:HEADS * HA],
                                          head_mask[:].rearrange("p h e -> p (h e)"), ALU.mult
                                          ).then_inc(state_ready, 1)
                    dve.wait_ge(dve_step, inverted)
                    if n >= 1:
                        dve.wait_ge(q_o_transposed, g * (GT + 1) + t + min(t, 1))
                    dve.tensor_tensor(attn_o[:].rearrange("p (h e) -> p h e", h=HEADS), num_den[:, :, 0:HD],
                                      den_inv[:].unsqueeze(2).broadcast_to([P, HEADS, HD]), ALU.mult
                                      ).then_inc(attn_o_ready, 1)

                for t in range(GT):
                    gap(t, 0)
                    apply(t)

            for q in range(GROUPS):
                route(q)
                shared(q)
            run_experts(0)
            split_biases()
            run_experts(1)
            for g in range(GROUPS):
                attend(g)
                route(GROUPS + g)
            run_experts(2)
            run_experts(3)
            shared(3)
            shared(2)
            for n in range(TILES // 4 - 1):
                q, j = GROUPS + n // QUADS, n % QUADS
                for k in range(TOPK - 1):
                    link(add_choice(q, j, k))
                add_choice(q, j, TOPK - 1).then_inc(x_final, 1)
            for i in range(4):
                dve.wait_ge(y_gathered_last[i], 16 * TOPK)
                for k in range(TOPK - 1):
                    link(add_tiles(2 * GROUPS - 1, QUADS - 1, k, (i,)))
                add_tiles(2 * GROUPS - 1, QUADS - 1, TOPK - 1, (i,)).then_inc(x_final, 1)


_INS = ['L0_attn_x', 'L0_attn_qkv_w', 'L0_attn_qkv_b', 'L0_attn_out_w', 'L0_attn_out_b',
        'L0_ffn_ws1', 'L0_ffn_bs1', 'L0_ffn_ws2', 'L0_ffn_bs2', 'L0_ffn_We1', 'L0_ffn_Be1',
        'L0_ffn_We2', 'L0_ffn_Be2', 'L0_ffn_Wr', 'L0_ffn_br']


def kernel(**inputs):
    import numpy as _np
    import concourse.bacc as _bacc
    from concourse import mybir as _mybir
    from concourse.bass_utils import run_bass_kernel_spmd as _run

    nc = _bacc.Bacc("TRN2", target_bir_lowering=False, num_devices=1)
    arrays, args = {}, []
    for name in _INS:
        a = _np.ascontiguousarray(inputs[name])
        arrays[f"in_{name}_dram"] = a
        args.append(nc.dram_tensor(f"in_{name}_dram", a.shape, _mybir.dt.from_np(a.dtype), kind="ExternalInput").ap())
    shape = inputs['L0_attn_x'].shape
    args.append(nc.dram_tensor("out_0_dram", shape, _mybir.dt.float32, kind="ExternalOutput").ap())
    macaron_kernel(nc, *args)
    r = _run(nc, [arrays], core_ids=[0])
    return r.results[0]["out_0_dram"]
```
